# Optimizing a Trainium2 kernel written in Bass

```python
import numpy as np
import jax
import jax.numpy as jnp

def _softmax(x, axis=-1):
    return jax.nn.softmax(x, axis=axis)

def _gelu(x):
    return jax.nn.gelu(x, approximate=True)

def _silu(x):
    return jax.nn.silu(x)

def _sigmoid(x):
    return jax.nn.sigmoid(x)

def _layernorm(x, axis=-1, eps=1e-05):
    m = jnp.mean(x, axis=axis, keepdims=True)
    v = jnp.var(x, axis=axis, keepdims=True)
    return (x - m) / jnp.sqrt(v + eps)

def _scatter_add(tgt, idx, src, axis=0):
    return tgt.at[idx].add(src)

def _segment_sum(src, seg, n):
    return jax.ops.segment_sum(src, seg, n)
kernel_name = 'mk_decoder_preln_d1_seqx_r4_aa304b'

def setup_inputs(seed: int=0):
    np.random.seed(seed)
    _w = jnp.asarray

    def _rec_inputs():
        import jax
        import jax.numpy as jnp
        _rk = jax.random.key(seed)
        x = 0.0003765 + 1 * jax.random.normal(jax.random.fold_in(_rk, 1), (16, 256, 512), jnp.float32)
        _lenS = 256 - jax.random.randint(jax.random.fold_in(_rk, 7), (16,), 0, max(1, 256 // 4) + 1, jnp.int32)
        _lenS2 = 256 - jax.random.randint(jax.random.fold_in(_rk, 8), (16,), 0, max(1, 256 // 4) + 1, jnp.int32)
        _ctx_2048P = jax.random.normal(jax.random.fold_in(_rk, 11), (16, 16, 512), jnp.float32)
        _ctx_2048c = jax.random.dirichlet(jax.random.fold_in(_rk, 511), 0.3 * jnp.ones((16,), jnp.float32), (16, 256))
        _ctx_2048t = jnp.einsum('bsk,bkd->bsd', _ctx_2048c, _ctx_2048P)
        _ctx_2048t = _ctx_2048t * jax.lax.rsqrt(jnp.mean(jnp.square(_ctx_2048t)) + 1e-12) * 0.953939
        ctx_2048 = -0.000292821 + 1.00034 * (_ctx_2048t + 0.3 * jax.random.normal(jax.random.fold_in(_rk, 611), (16, 256, 512), jnp.float32))
        return (x, ctx_2048)
    x, ctx_2048 = _rec_inputs()

    def _L0_attn_setup():
        import jax, jax.numpy as jnp
        import numpy as np
        import math
        B, T = (4, 256)
        D_MODEL = 512
        HEAD_DIM = 64
        N_HEADS = 32
        N_KV = 8
        Q_MULT = N_HEADS // N_KV
        SLIDING_WINDOW = 128
        CAUSAL = True
        SM_SCALE = 1.0 / math.sqrt(HEAD_DIM)
        ROPE_THETA = 150000.0
        SCALING = 32.0
        NTK_ALPHA = 1.0
        NTK_BETA = 32.0
        ICL = 256

        def _rope_cos_sin(t_len):
            d_half = HEAD_DIM // 2
            freq = ROPE_THETA ** (np.arange(0, HEAD_DIM, 2, dtype=np.float32) / HEAD_DIM)
            concentration = 0.1 * math.log(SCALING) + 1.0
            low = d_half * math.log(ICL / (NTK_BETA * 2 * math.pi)) / math.log(ROPE_THETA)
            high = d_half * math.log(ICL / (NTK_ALPHA * 2 * math.pi)) / math.log(ROPE_THETA)
            interpolation = 1.0 / (SCALING * freq)
            extrapolation = 1.0 / freq
            ramp = np.clip((np.arange(d_half, dtype=np.float32) - low) / (high - low), 0.0, 1.0)
            mask = 1.0 - ramp
            inv_freq = interpolation * (1.0 - mask) + extrapolation * mask
            freqs = np.outer(np.arange(t_len, dtype=np.float32), inv_freq)
            return (jnp.asarray(np.cos(freqs) * concentration, jnp.float32), jnp.asarray(np.sin(freqs) * concentration, jnp.float32))

        def _apply_rope(x, cos, sin):
            x1, x2 = jnp.split(x, 2, axis=-1)
            return jnp.concatenate([x1 * cos - x2 * sin, x2 * cos + x1 * sin], axis=-1)
        key = jax.random.key(seed)
        ks = jax.random.split(key, 6)
        qkv_dim = HEAD_DIM * (N_HEADS + 2 * N_KV)
        return {'x': jax.random.normal(ks[0], (B, T, D_MODEL), jnp.float32), 'qkv_w': jax.random.normal(ks[1], (qkv_dim, D_MODEL), jnp.float32) * 0.02, 'qkv_b': jax.random.normal(ks[2], (qkv_dim,), jnp.float32) * 0.02, 'out_w': jax.random.normal(ks[3], (D_MODEL, N_HEADS * HEAD_DIM), jnp.float32) * 0.02, 'out_b': jax.random.normal(ks[4], (D_MODEL,), jnp.float32) * 0.02, 'sinks': jax.random.normal(ks[5], (N_HEADS,), jnp.float32) * (1.0 / math.sqrt(HEAD_DIM))}
    _L0_attn_all = _L0_attn_setup()
    _L0_attn_in = {k: v for k, v in _L0_attn_all.items() if k in ('qkv_w', 'qkv_b', 'out_w', 'out_b', 'sinks')}
    del _L0_attn_all

    def _L0_xattn_setup():
        import jax, jax.numpy as jnp
        import numpy as np
        key = jax.random.key(seed)
        k1, k2, k3, k4, k5 = jax.random.split(key, 5)
        B, D_MODEL, L = (2, 256, 512)
        HEAD_DIM = 8
        H = D_MODEL // HEAD_DIM
        return {'k': jax.random.normal(k1, (B, D_MODEL, L), dtype=jnp.float32), 'v': jax.random.normal(k2, (B, D_MODEL, L), dtype=jnp.float32), 'q': jax.random.normal(k3, (B, D_MODEL, L), dtype=jnp.float32), 'ssm_kernel': jax.random.normal(k4, (H, L), dtype=jnp.float32), 'D': jax.random.normal(k5, (H,), dtype=jnp.float32), 'head_dim': HEAD_DIM}
    _L0_xattn_all = _L0_xattn_setup()
    _L0_xattn_in = {k: v for k, v in _L0_xattn_all.items() if k in ('ssm_kernel', 'D')}
    del _L0_xattn_all

    def _L0_ffn_setup():
        import math
        import jax, jax.numpy as jnp
        import numpy as np
        DIM = 512
        RANK = 8
        B, T = (4, 1024)

        def _orthogonal(key, n):
            a = jax.random.normal(key, (n, n), dtype=jnp.float32)
            q, r = jnp.linalg.qr(a)
            q = q * jnp.sign(jnp.diagonal(r))[None, :]
            return q
        key = jax.random.key(seed)
        kx, kf = jax.random.split(key)
        x = jax.random.normal(kx, (B, T, DIM), dtype=jnp.float32)
        fkeys = jax.random.split(kf, RANK)
        factors = jnp.stack([_orthogonal(fkeys[r], DIM) * (r + 1) ** (-0.5) for r in range(RANK)])
        bias = jnp.zeros((DIM,), dtype=jnp.float32)
        return {'x': x, 'factors': factors, 'bias': bias}
    _L0_ffn_all = _L0_ffn_setup()
    _L0_ffn_in = {k: v for k, v in _L0_ffn_all.items() if k in ('factors', 'bias')}
    del _L0_ffn_all
    return {'x': x, 'ctx_2048': ctx_2048, 'L0_attn_qkv_w': _L0_attn_in['qkv_w'], 'L0_attn_qkv_b': _L0_attn_in['qkv_b'], 'L0_attn_out_w': _L0_attn_in['out_w'], 'L0_attn_out_b': _L0_attn_in['out_b'], 'L0_attn_sinks': _L0_attn_in['sinks'], 'L0_xattn_ssm_kernel': _L0_xattn_in['ssm_kernel'], 'L0_xattn_D': _L0_xattn_in['D'], 'L0_ffn_factors': _L0_ffn_in['factors'], 'L0_ffn_bias': _L0_ffn_in['bias']}

def reference(x, ctx_2048, L0_attn_qkv_w, L0_attn_qkv_b, L0_attn_out_w, L0_attn_out_b, L0_attn_sinks, L0_xattn_ssm_kernel, L0_xattn_D, L0_ffn_factors, L0_ffn_bias):
    import jax
    import jax.numpy as jnp

    def _L0_attn_ref(x, qkv_w, qkv_b, out_w, out_b, sinks):
        import jax, jax.numpy as jnp
        import numpy as np
        import math
        B, T = (4, 256)
        D_MODEL = 512
        HEAD_DIM = 64
        N_HEADS = 32
        N_KV = 8
        Q_MULT = N_HEADS // N_KV
        SLIDING_WINDOW = 128
        CAUSAL = True
        SM_SCALE = 1.0 / math.sqrt(HEAD_DIM)
        ROPE_THETA = 150000.0
        SCALING = 32.0
        NTK_ALPHA = 1.0
        NTK_BETA = 32.0
        ICL = 256

        def _rope_cos_sin(t_len):
            d_half = HEAD_DIM // 2
            freq = ROPE_THETA ** (np.arange(0, HEAD_DIM, 2, dtype=np.float32) / HEAD_DIM)
            concentration = 0.1 * math.log(SCALING) + 1.0
            low = d_half * math.log(ICL / (NTK_BETA * 2 * math.pi)) / math.log(ROPE_THETA)
            high = d_half * math.log(ICL / (NTK_ALPHA * 2 * math.pi)) / math.log(ROPE_THETA)
            interpolation = 1.0 / (SCALING * freq)
            extrapolation = 1.0 / freq
            ramp = np.clip((np.arange(d_half, dtype=np.float32) - low) / (high - low), 0.0, 1.0)
            mask = 1.0 - ramp
            inv_freq = interpolation * (1.0 - mask) + extrapolation * mask
            freqs = np.outer(np.arange(t_len, dtype=np.float32), inv_freq)
            return (jnp.asarray(np.cos(freqs) * concentration, jnp.float32), jnp.asarray(np.sin(freqs) * concentration, jnp.float32))

        def _apply_rope(x, cos, sin):
            x1, x2 = jnp.split(x, 2, axis=-1)
            return jnp.concatenate([x1 * cos - x2 * sin, x2 * cos + x1 * sin], axis=-1)
        Bv, Tv, _ = x.shape
        qkv = x @ qkv_w.T + qkv_b
        q = qkv[..., :N_HEADS * HEAD_DIM].reshape(Bv, Tv, N_KV, Q_MULT, HEAD_DIM)
        k = qkv[..., N_HEADS * HEAD_DIM:(N_HEADS + N_KV) * HEAD_DIM].reshape(Bv, Tv, N_KV, HEAD_DIM)
        v = qkv[..., (N_HEADS + N_KV) * HEAD_DIM:].reshape(Bv, Tv, N_KV, HEAD_DIM)
        cos, sin = _rope_cos_sin(Tv)
        q = _apply_rope(q, cos[:, None, None, :], sin[:, None, None, :])
        k = _apply_rope(k, cos[:, None, :], sin[:, None, :])
        logits = jnp.einsum('bqhmd,bkhd->bhmqk', q, k) * SM_SCALE
        i = jnp.arange(Tv)[:, None]
        j = jnp.arange(Tv)[None, :]
        mask = jnp.zeros((Tv, Tv), dtype=bool)
        if CAUSAL:
            mask = mask | (j > i)
        if SLIDING_WINDOW > 0:
            mask = mask | (j <= i - SLIDING_WINDOW)
        logits = jnp.where(mask, -jnp.inf, logits)
        m = jnp.max(logits, axis=-1, keepdims=True)
        e = jnp.exp(logits - m)
        s = sinks.reshape(N_KV, Q_MULT)[None, :, :, None, None]
        exp_sink = jnp.exp(s - m)
        w = e / (jnp.sum(e, axis=-1, keepdims=True) + exp_sink)
        out = jnp.einsum('bhmqk,bkhd->bqhmd', w, v).reshape(Bv, Tv, N_HEADS * HEAD_DIM)
        return out @ out_w.T + out_b

    def _L0_xattn_ref(k, v, q, ssm_kernel, D, head_dim):
        import jax, jax.numpy as jnp
        import numpy as np
        B, HD, L = k.shape
        H = HD // head_dim
        fft_size = 2 * L
        k_ = k.reshape(B, H, head_dim, L)
        v_ = v.reshape(B, H, head_dim, L)
        q_ = q.reshape(B, H, head_dim, L)
        kv = jnp.einsum('bhil,bhjl->bijhl', k_, v_)
        kv_f = jnp.fft.rfft(kv, n=fft_size)
        kernel_f = jnp.fft.rfft(ssm_kernel, n=fft_size)
        y = jnp.fft.irfft(kv_f * kernel_f, n=fft_size)[..., :L]
        out = y + kv * D[None, None, None, :, None]
        out = jnp.einsum('bijhl,bhil->bjhl', out, q_)
        out = jnp.transpose(out, (0, 2, 1, 3)).reshape(B, H * head_dim, L)
        return out.astype(k.dtype)

    def _L0_ffn_ref(x, factors, bias):
        import math
        import jax, jax.numpy as jnp
        import numpy as np
        DIM = 512
        RANK = 8
        B, T = (4, 1024)

        def _orthogonal(key, n):
            a = jax.random.normal(key, (n, n), dtype=jnp.float32)
            q, r = jnp.linalg.qr(a)
            q = q * jnp.sign(jnp.diagonal(r))[None, :]
            return q
        rank = factors.shape[0]
        mixed = jnp.einsum('btd,rde->bte', x, factors)
        mixed = mixed / math.sqrt(rank) + bias
        return mixed
    x = x + _L0_attn_ref(_layernorm(x, axis=-1), L0_attn_qkv_w, L0_attn_qkv_b, L0_attn_out_w, L0_attn_out_b, L0_attn_sinks)
    x = x + _L0_xattn_ref(ctx_2048, ctx_2048, _layernorm(x, axis=-1), L0_xattn_ssm_kernel, L0_xattn_D, 8)
    x = x + _L0_ffn_ref(_layernorm(x, axis=-1), L0_ffn_factors, L0_ffn_bias)
    return x

_drawn_inputs = setup_inputs


def setup_inputs(seed=0):
    import zlib

    import numpy as np

    out = dict(_drawn_inputs(seed))
    spreads = {'L0_ffn_bias': (0.0, 2.0)}
    factors = {'L0_attn_sinks': 42.323, 'L0_ffn_factors': 5.397}
    for name, (base, spread) in spreads.items():
        noise = np.random.default_rng([zlib.crc32(name.encode()), seed]).standard_normal(out[name].shape)
        drawn = base * np.exp(spread * noise) if base else spread * noise
        out[name] = jnp.asarray(drawn.astype(out[name].dtype))
    for name, factor in factors.items():
        out[name] = (out[name] * factor).astype(out[name].dtype)
    return out
```

```python
import math
from contextlib import ExitStack

import numpy as np

import concourse.bass as bass
from concourse import mybir

F32 = mybir.dt.float32
ALU = mybir.AluOpType
ACT = mybir.ActivationFunctionType
AX = mybir.AxisListType

P = 128
B, T, D = 16, 256, 512
NT = T // P
KD = D // P
HD = 64
NKV, QM = 8, 4
NH = NKV * QM
GW = (QM + 2) * HD
RW = (QM + 1) * HD
SM_SCALE = 1.0 / math.sqrt(HD)
MASKED = -1.0e30
EPS = 1e-5
SK = P + T

CH, CD = 32, 8
RANK = 8
NPAIR = CD * (CD + 1) // 2
BG = 8
NBG = B // BG
NY = BG * NPAIR
PADW = P + D


def rope_tables():
    theta, scaling, alpha, beta, icl = 150000.0, 32.0, 1.0, 32.0, 256
    half = HD // 2
    freq = theta ** (np.arange(0, HD, 2, dtype=np.float32) / HD)
    conc = 0.1 * math.log(scaling) + 1.0
    low = half * math.log(icl / (beta * 2 * math.pi)) / math.log(theta)
    high = half * math.log(icl / (alpha * 2 * math.pi)) / math.log(theta)
    ramp = np.clip((np.arange(half, dtype=np.float32) - low) / (high - low), 0.0, 1.0)
    mask = 1.0 - ramp
    inv = 1.0 / (scaling * freq) * (1.0 - mask) + 1.0 / freq * mask
    ang = np.outer(np.arange(T, dtype=np.float32), inv)
    cos = (np.cos(ang) * conc).astype(np.float32)
    sin = (np.sin(ang) * conc).astype(np.float32)
    tab = np.concatenate([cos, cos, -sin, sin], axis=1).reshape(NT, P, 2 * HD)
    return np.ascontiguousarray(tab.transpose(1, 0, 2))


def score_masks():
    q, k = np.arange(P)[:, None], np.arange(P)[None, :]
    same = np.where(k > q, MASKED, 0.0)
    before = np.where(k <= q, MASKED, 0.0)
    return np.concatenate([same, before, same], axis=1).astype(np.float32)


def wait_apart(eng, passed, *waits):
    for s, v in waits:
        if not isinstance(v, int) or v > 0:
            eng.wait_ge(s, v)
    eng.sem_inc(passed, 1)


def attention_part(nc, x, wqkv, bqkv, wout, bout, sinks, rope, masks, ident, x1_dram, q2_dram):
    with ExitStack() as ctx:
        def sb(name, shape):
            return ctx.enter_context(nc.sbuf_tensor(name, shape, F32))

        def ps(name):
            return ctx.enter_context(nc.psum_tensor(name, [P, 512], F32))

        def sem(name):
            return ctx.enter_context(nc.semaphore(name))

        w_sb = sb("w_sb", [P, KD, NKV, GW])
        wo_sb = sb("wo_sb", [P, NH * HD // P, D])
        bias_sb = sb("bias_sb", [P, NKV, GW])
        bo_sb = sb("bo_sb", [P, D])
        sink_sb = sb("sink_sb", [P, NH])
        rope_sb = sb("rope_sb", [P, NT, 2, HD])
        mask_sb = sb("mask_sb", [P, SK])
        id_sb = sb("id_sb", [P, P])
        x_in = sb("x_in", [P, NT, D])
        xn = sb("xn", [P, NT, D])
        xnT = sb("xnT", [P, NT, KD, P])
        stats = sb("stats", [P, NT, 6])
        mv = sb("mv", [P, NT, 2])
        veps = sb("veps", [P, NT])
        rstd = sb("rstd", [P, NT])
        mhalf = sb("mhalf", [P, NT])
        qk = sb("qk", [P, 2, QM + 1, HD])
        m1 = sb("m1", [P, 2, QM + 1, HD])
        m2 = sb("m2", [P, 2, QM + 1, HD])
        qr = sb("qr", [P, 2, QM + 2, HD])
        vv = sb("vv", [P, NKV, NT, HD + 1])
        qT = sb("qT", [P, 2, 3, T])
        pr = sb("pr", [P, 4, 2, SK])
        mx = sb("mx", [P, 4, 2 * NT])
        nm = sb("nm", [P, 4, 2 * NT])
        sk = sb("sk", [P, 4, 2 * NT])
        es = sb("es", [P, 4, 2 * NT])
        pT = sb("pT", [P, 2, 2, SK])
        den = sb("den", [P, 2 * NT])
        rden = sb("rden", [P, 2 * NT])
        o_sb = sb("o_sb", [P, 2, NT, QM, HD])
        oT = sb("oT", [P, 2, NT, 2, P])
        xb = sb("xb", [P, NT, D])
        x1 = sb("x1", [P, NT, D])
        x1n = sb("x1n", [P, NT, D])
        x1T = sb("x1T", [P, KD, T])
        st2 = sb("st2", [P, NT, 6])
        mv2 = sb("mv2", [P, NT, 2])
        ve2 = sb("ve2", [P, NT])
        rs2 = sb("rs2", [P, NT])

        wP = ps("wP")
        tP = ps("tP")
        sP = [ps("sP0"), ps("sP1")]
        pP = ps("pP")
        vP = ps("vP")
        oP = [ps("oP0"), ps("oP1")]

        c_in = sem("c_in")
        mask_landed = sem("mask_landed")
        passed = sem("passed")
        x_landed = sem("x_landed")
        xb_landed = sem("xb_landed")
        mhalf_set = sem("mhalf_set")
        ones_set = sem("ones_set")
        ln_chain = sem("ln_chain")
        ve_ready = sem("ve_ready")
        rstd_ready = sem("rstd_ready")
        xn_ready = sem("xn_ready")
        xt_done = sem("xt_done")
        xt_evac = sem("xt_evac")
        qkv_done = sem("qkv_done")
        qk_ready = sem("qk_ready")
        v_ready = sem("v_ready")
        m1_ready = sem("m1_ready")
        m2_ready = sem("m2_ready")
        qr_ready = sem("qr_ready")
        qt_done = sem("qt_done")
        qt_evac = sem("qt_evac")
        s_done = sem("s_done")
        masked = sem("masked")
        nm_ready = sem("nm_ready")
        sk_ready = sem("sk_ready")
        exp_done = sem("exp_done")
        es_ready = sem("es_ready")
        pt_done = sem("pt_done")
        pt_evac0 = sem("pt_evac0")
        pt_evac1 = sem("pt_evac1")
        pv_done = sem("pv_done")
        den_ready = sem("den_ready")
        rden_ready = sem("rden_ready")
        o_ready = sem("o_ready")
        ot_done = sem("ot_done")
        ot_evac = sem("ot_evac")
        out_done = sem("out_done")
        xb_ready = sem("xb_ready")
        x1_ready = sem("x1_ready")
        ln2_chain = sem("ln2_chain")
        ve2_ready = sem("ve2_ready")
        rs2_ready = sem("rs2_ready")
        x1n_ready = sem("x1n_ready")
        x1t_done = sem("x1t_done")
        x1t_evac = sem("x1t_evac")
        x1_stored = sem("x1_stored")
        x1t_stored = sem("x1t_stored")

        block = ctx.enter_context(nc.Block())
        NCONST = 7

        def wait(eng, s, value):
            if isinstance(value, int) and value <= 0:
                return
            eng.wait_ge(s, value)

        def batches(eng, body):
            body(0, first=True)
            body(1)
            with eng.Fori(2, B - 1) as b:
                body(b)
            body(B - 1, last=True)
            body(B, drain=True)

        def lagged(b, g, lag, first, drain):
            n = g - lag
            return not (first and n < 0) and not (drain and n >= 0)

        @block.sync
        def _(sp):
            sp.dma_start(x_in[:], x[0].rearrange("(t p) d -> p t d", p=P)).then_inc(x_landed, 16)
            sp.dma_start(id_sb[:], ident).then_inc(c_in, 16)
            sp.dma_start(w_sb[:], wqkv).then_inc(c_in, 16)
            sp.dma_start(bias_sb[:].rearrange("p g n -> p (g n)"), bqkv.partition_broadcast(P)).then_inc(c_in, 16)
            sp.dma_start(rope_sb[:].rearrange("p t a d -> p t (a d)"), rope).then_inc(c_in, 16)
            sp.dma_start(mask_sb[:], masks).then_inc(mask_landed, 16)
            sp.dma_start(sink_sb[:], sinks.partition_broadcast(P)).then_inc(c_in, 16)
            sp.dma_start(bo_sb[:], bout.partition_broadcast(P)).then_inc(c_in, 16)
            sp.dma_start(wo_sb[:], wout).then_inc(c_in, 16)

            def body(b, first=False, last=False, drain=False):
                if not (last or drain):
                    sp.wait_ge(xn_ready, 2 * b + 2)
                    sp.dma_start(x_in[:], x[b + 1].rearrange("(t p) d -> p t d", p=P)).then_inc(x_landed, 16)
                if not drain:
                    wait(sp, x1_ready, 2 * b)
                    sp.dma_start(xb[:], x[b].rearrange("(t p) d -> p t d", p=P)).then_inc(xb_landed, 16)
                if not first:
                    sp.wait_ge(x1_ready, 2 * b)
                    sp.dma_start(x1_dram[b - 1].rearrange("(t p) d -> p t d", p=P), x1[:]).then_inc(x1_stored, 16)
                    sp.wait_ge(x1t_evac, 2 * b)
                    sp.dma_start(q2_dram[b - 1], x1T[:]).then_inc(x1t_stored, 16)
            batches(sp, body)
            sp.wait_ge(x1_stored, 16 * B)
            sp.wait_ge(x1t_stored, 16 * B)

        @block.tensor
        def _(pe):
            pe.wait_ge(c_in, 16 * NCONST)

            def x_transposes(b, j):
                wait(pe, qt_evac, 16 * b - 2 + j)
                if j == 1:
                    pe.wait_ge(xt_evac, 2 * b + 1)
                wait(pe, ot_evac, 8 * b - 4)
                pe.wait_ge(xn_ready, 2 * b + j + 1)
                for c in range(KD):
                    last = pe.transpose(tP[:, c * P:(c + 1) * P], xn[:, j, c * P:(c + 1) * P], id_sb[:])
                last.then_inc(xt_done, 1)

            def qkv(b, g, j):
                pe.wait_ge(xt_evac, 2 * b + j + 1)
                wait(pe, qk_ready, 16 * b + 2 * g + j)
                wait(pe, v_ready, 16 * b + 2 * g + j)
                for c in range(KD):
                    last = pe.matmul(wP[:, 0:GW], xnT[:, j, c, :], w_sb[:, c, g, :],
                                     start=(c == 0), stop=(c == KD - 1))
                last.then_inc(qkv_done, 1)

            def q_transposes(b, g, j, drain):
                h = 16 * b + 2 * g + j
                pe.wait_ge(qr_ready, h + 1)
                wait(pe, qt_evac, h)
                if g == -1 and not drain:
                    pe.wait_ge(xt_evac, 2 * b + j + 1)
                if j == 0:
                    wait(pe, ot_evac, 8 * b + g - 3)
                if g == 6 and j == 0:
                    wait(pe, x1t_evac, 2 * b)
                if g == 5 and j == 1:
                    wait(pe, x1t_evac, 2 * b - 1)
                for c in range(3):
                    last = pe.transpose(tP[:, c * P:(c + 1) * P],
                                        qr[:, j, 2 * c:2 * c + 2, :].rearrange("p a d -> p (a d)"), id_sb[:])
                last.then_inc(qt_done, 1)

            def scores(b, g, j):
                h = 16 * b + 2 * g + j
                pe.wait_ge(qt_evac, 16 * b + 2 * g + 2)
                wait(pe, masked, h)
                for a in range(2):
                    r = slice(a * HD, a * HD + HD)
                    for t in range(NT):
                        k0 = t * P
                        last = pe.matmul(sP[a][:, k0:P + 2 * k0], qT[r, g % 2, j, t * P:(t + 1) * P],
                                         qT[r, g % 2, 2, 0:(t + 1) * P], start=True, stop=True)
                last.then_inc(s_done, 1)

            def p_transposes(b, g, j, a):
                h = 16 * b + 2 * g + j
                pe.wait_ge(exp_done, 2 * h + a + 1)
                if a == 0:
                    wait(pe, pt_evac1, h)
                else:
                    pe.wait_ge(pt_evac0, h + 1)
                for c in range(3):
                    last = pe.transpose(pP[:, c * P:(c + 1) * P], pr[:, (2 * g + j) % 4, a, c * P:(c + 1) * P], id_sb[:])
                last.then_inc(pt_done, 1)

            def pv(b, g, j):
                h = 16 * b + 2 * g + j
                s = (2 * g + j) % 2
                pe.wait_ge(pt_evac0, h + 1)
                pe.wait_ge(pt_evac1, h + 1)
                wait(pe, o_ready, h)
                pe.wait_ge(v_ready, 16 * b + 2 * g + 2)
                pe.wait_ge(ones_set, 1)
                for a in range(2):
                    o = vP[:, a * P * 2:a * P * 2 + HD + 1]
                    pe.matmul(o, pT[:, s, a, 0:P], vv[:, g % NKV, 0, :], start=True, stop=True)
                    o = vP[:, a * P * 2 + P:a * P * 2 + P + HD + 1]
                    pe.matmul(o, pT[:, s, a, P:2 * P], vv[:, g % NKV, 0, :], start=True, stop=False)
                    last = pe.matmul(o, pT[:, s, a, 2 * P:3 * P], vv[:, g % NKV, 1, :], start=False, stop=True)
                last.then_inc(pv_done, 1)

            def o_transposes(b, g, drain):
                pe.wait_ge(o_ready, 16 * b + 2 * g + 2)
                pe.wait_ge(qt_evac, 16 * B if drain else 16 * b + 2 * g + 8)
                wait(pe, ot_evac, 8 * b + g)
                for t in range(NT):
                    for c in range(2):
                        last = pe.transpose(tP[:, (2 * t + c) * P:(2 * t + c + 1) * P],
                                            o_sb[:, g % 2, t, 2 * c:2 * c + 2, :].rearrange("p a d -> p (a d)"), id_sb[:])
                last.then_inc(ot_done, 1)

            def out_projection(b, g, j):
                gg = g % NKV
                pe.wait_ge(ot_evac, 8 * b + g + 1)
                if gg == 0:
                    wait(pe, x1_ready, 2 * b - 1 + j)
                for c in range(2):
                    last = pe.matmul(oP[j][:], oT[:, gg % 2, j, c, :], wo_sb[:, 2 * gg + c, :],
                                     start=(gg == 0 and c == 0), stop=(gg == NKV - 1 and c == 1))
                last.then_inc(out_done, 1)

            def x1_transposes(b, j, drain):
                pe.wait_ge(x1n_ready, 2 * b - 1 + j)
                if drain:
                    pe.wait_ge(ot_evac, 8 * b)
                else:
                    pe.wait_ge(qt_evac, 16 * b + 11 + j)
                    pe.wait_ge(ot_evac, 8 * b + 2 + j)
                if j == 1:
                    pe.wait_ge(x1t_evac, 2 * b - 1)
                for c in range(KD):
                    last = pe.transpose(tP[:, c * P:(c + 1) * P], x1n[:, j, c * P:(c + 1) * P], id_sb[:])
                last.then_inc(x1t_done, 1)

            def body(b, first=False, last=False, drain=False):
                for g in range(NKV):
                    for j in range(2):
                        here = not drain
                        if g == 0 and here:
                            x_transposes(b, j)
                        if lagged(b, g, 3, first, drain):
                            p_transposes(b, g - 3, j, 0)
                        if g > 0 and here:
                            qkv(b, g, j)
                        if lagged(b, g, 3, first, drain):
                            p_transposes(b, g - 3, j, 1)
                        if lagged(b, g, 1, first, drain):
                            q_transposes(b, g - 1, j, drain)
                        if lagged(b, g, 2, first, drain):
                            scores(b, g - 2, j)
                        gg, jj = (g - 4, 1) if j == 0 else (g - 3, 0)
                        if lagged(b, 0, -gg, first, drain):
                            pv(b, gg, jj)
                        if g == 0 and here:
                            qkv(b, g, j)
                        if j == 1 and lagged(b, g, 4, first, drain):
                            o_transposes(b, g - 4, drain)
                        if lagged(b, g, 5, first, drain):
                            out_projection(b, g - 5, j)
                        if g == 6 and not first:
                            x1_transposes(b, j, drain)
            batches(pe, body)

        @block.scalar
        def _(act):
            def x_evac(b, j):
                act.wait_ge(xt_done, 2 * b + j + 1)
                wait(act, qkv_done, 16 * b)
                act.copy(xnT[:, j], tP[:, 0:D].rearrange("p (c t) -> p c t", c=KD)).then_inc(xt_evac, 1)

            def q_evac(b, g, j):
                h = 16 * b + 2 * g + j
                act.wait_ge(qt_done, h + 1)
                wait(act, s_done, 16 * b + 2 * g - 2)
                act.copy(qT[:, g % 2, :, j * P:(j + 1) * P],
                         tP[:, 0:3 * P].rearrange("p (c t) -> p c t", c=3)).then_inc(qt_evac, 1)

            def exps(b, g, j):
                h = 16 * b + 2 * g + j
                s = (2 * g + j) % 4
                act.wait_ge(nm_ready, h + 1)
                for a in range(2):
                    for t in range(NT):
                        cols = slice(t * P, P + 2 * t * P)
                        last = act.activation(pr[:, s, a, cols], pr[:, s, a, cols], ACT.Exp,
                                              bias=nm[:, s, 2 * a + t:2 * a + t + 1], scale=SM_SCALE)
                    last.then_inc(exp_done, 1)
                act.wait_ge(sk_ready, h + 1)
                wait(act, den_ready, h - 3)
                act.activation(es[:, s, :], sk[:, s, :], ACT.Exp).then_inc(es_ready, 1)

            def p_evac(b, g, j):
                h = 16 * b + 2 * g + j
                act.wait_ge(pt_done, 2 * h + 1)
                wait(act, pv_done, h - 1)
                act.copy(pT[:, (2 * g + j) % 2, 0, :], pP[:, 0:SK]).then_inc(pt_evac0, 1)

            def o_evac(b, g):
                act.wait_ge(ot_done, 8 * b + g + 1)
                wait(act, out_done, 16 * b + 2 * g - 2)
                act.copy(oT[:, g % 2].rearrange("p t c n -> p (t c n)"), tP[:, 0:512]).then_inc(ot_evac, 1)

            def x1_evac(b, j):
                act.wait_ge(x1t_done, 2 * b - 1 + j)
                wait(act, x1t_stored, 16 * (b - 1))
                act.copy(x1T[:, :, j * P:(j + 1) * P], tP[:, 0:D].rearrange("p (c t) -> p c t", c=KD)).then_inc(x1t_evac, 1)

            def body(b, first=False, last=False, drain=False):
                for g in range(NKV):
                    for j in range(2):
                        if g == 0 and not drain:
                            x_evac(b, j)
                        if lagged(b, g, 3, first, drain):
                            p_evac(b, g - 3, j)
                        if lagged(b, g, 1, first, drain):
                            q_evac(b, g - 1, j)
                        if lagged(b, g, 2, first, drain):
                            exps(b, g - 2, j)
                        if j == 1 and lagged(b, g, 4, first, drain):
                            o_evac(b, g - 4)
                        if g == 6 and not first:
                            x1_evac(b, j)
            batches(act, body)

        @block.gpsimd
        def _(pool):
            pool.memset(mhalf[:], -0.5).then_inc(mhalf_set, 1)
            pool.memset(vv[:, :, :, HD:HD + 1], 1.0).then_inc(ones_set, 1)
            pool.wait_ge(mhalf_set, 1)
            pool.wait_ge(c_in, 16 * NCONST)

            def power(src, dst, ready, done, n):
                pool.wait_ge(ready, n)
                pool.tensor_tensor(dst[:], src[:], mhalf[:], ALU.pow).then_inc(done, 1)

            def sin_part(b, g, j):
                h = 16 * b + 2 * g + j
                pool.wait_ge(qk_ready, h + 1)
                wait(pool, qr_ready, h - 1)
                half = HD // 2
                for s in range(2):
                    d, o = s * half, (1 - s) * half
                    last = pool.tensor_tensor(m2[:, j, :, d:d + half], qk[:, j, :, o:o + half],
                                              rope_sb[:, j, 1:2, d:d + half].broadcast_to([P, QM + 1, half]), ALU.mult)
                last.then_inc(m2_ready, 1)

            power(veps, rstd, ve_ready, rstd_ready, 1)

            def body(b, first=False, last=False, drain=False):
                for g in range(NKV):
                    for j in range(2):
                        if not drain:
                            sin_part(b, g, j)
                    if g == 7 and not drain:
                        pool.wait_ge(xb_landed, 16 * b + 16)
                        for t in range(NT):
                            last = pool.tensor_tensor(xb[:, t, :], xb[:, t, :], bo_sb[:], ALU.add)
                        last.then_inc(xb_ready, 1)
                    if g == 4 and not first:
                        power(ve2, rs2, ve2_ready, rs2_ready, b)
                    if g == 5 and not (last or drain):
                        power(veps, rstd, ve_ready, rstd_ready, b + 2)
            batches(pool, body)

        @block.vector
        def _(dve):
            def layernorm_start(src, st, mvv, ve, chain, n, ready):
                for t in range(NT):
                    last = dve.bn_stats(st[:, t, :], src[:, t, :])
                last.then_inc(chain, 1)
                wait_apart(dve, passed, (chain, n + 1))
                for t in range(NT):
                    last = dve.bn_aggr(mvv[:, t, :], st[:, t, :])
                last.then_inc(chain, 1)
                dve.wait_ge(chain, n + 2)
                dve.tensor_scalar(ve[:], mvv[:, :, 1], EPS, None, ALU.add).then_inc(ready, 1)

            def layernorm_end(dst, src, mvv, rs, done):
                for t in range(NT):
                    dve.tensor_scalar(dst[:, t, :], src[:, t, :], mvv[:, t, 0:1], rs[:, t:t + 1],
                                      ALU.subtract, ALU.mult).then_inc(done, 1)

            def ln1_start(b):
                dve.wait_ge(x_landed, 16 * b + 16)
                layernorm_start(x_in, stats, mv, veps, ln_chain, 2 * b, ve_ready)

            def ln1_end(b):
                dve.wait_ge(rstd_ready, b + 1)
                wait(dve, xt_done, 2 * b)
                layernorm_end(xn, x_in, mv, rstd, xn_ready)

            def qkv_evac(b, g, j):
                h = 16 * b + 2 * g + j
                dve.wait_ge(qkv_done, h + 1)
                wait(dve, m2_ready, h - 1)
                dve.tensor_tensor(qk[:, j].rearrange("p a d -> p (a d)"), wP[:, 0:RW], bias_sb[:, g, 0:RW],
                                  ALU.add).then_inc(qk_ready, 1)
                wait(dve, pv_done, h - j - 14)
                dve.tensor_tensor(vv[:, g, j, 0:HD], wP[:, RW:GW], bias_sb[:, g, RW:GW], ALU.add).then_inc(v_ready, 1)

            def cos_part(b, g, j):
                h = 16 * b + 2 * g + j
                dve.wait_ge(qk_ready, h + 1)
                wait(dve, qr_ready, h - 1)
                dve.tensor_tensor(m1[:, j], qk[:, j], rope_sb[:, j, 0:1, :].broadcast_to([P, QM + 1, HD]),
                                  ALU.mult).then_inc(m1_ready, 1)

            def rotate(b, g, j):
                h = 16 * b + 2 * g + j
                dve.wait_ge(m1_ready, h + 1)
                dve.wait_ge(m2_ready, h + 1)
                wait(dve, qt_done, h - 1)
                dve.tensor_tensor(qr[:, j, 0:QM], m1[:, j, 0:QM], m2[:, j, 0:QM], ALU.add)
                dve.tensor_tensor(qr[:, j, QM:QM + 2], m1[:, j, QM:QM + 1].broadcast_to([P, 2, HD]),
                                  m2[:, j, QM:QM + 1].broadcast_to([P, 2, HD]), ALU.add).then_inc(qr_ready, 1)

            def p_evac(b, g, j):
                h = 16 * b + 2 * g + j
                dve.wait_ge(pt_done, 2 * h + 2)
                wait(dve, pv_done, h - 1)
                dve.tensor_copy(pT[:, (2 * g + j) % 2, 1, :], pP[:, 0:SK]).then_inc(pt_evac1, 1)

            def mask_max(b, g, j):
                h = 16 * b + 2 * g + j
                s = (2 * g + j) % 4
                wait_apart(dve, passed, (mask_landed, 16), (s_done, h + 1), (pt_done, 2 * (h - 3)), (es_ready, h - 3))
                for a in range(2):
                    for t in range(NT):
                        cols = slice(t * P, P + 2 * t * P)
                        last = dve.tensor_tensor_reduce(pr[:, s, a, cols], sP[a][:, cols], mask_sb[:, cols], 1.0, -3.0e38,
                                                        ALU.add, ALU.max, mx[:, s, 2 * a + t:2 * a + t + 1])
                last.then_inc(masked, 1)
                dve.wait_ge(masked, h + 1)
                dve.tensor_scalar(nm[:, s, :], mx[:, s, :], -SM_SCALE, None, ALU.mult).then_inc(nm_ready, 1)
                dve.wait_ge(nm_ready, h + 1)
                head = QM * (g % NKV) + 2 * j
                dve.tensor_tensor(sk[:, s, :].rearrange("p (a t) -> p a t", a=2), nm[:, s, :].rearrange("p (a t) -> p a t", a=2),
                                  sink_sb[:, head:head + 2].unsqueeze(2).broadcast_to([P, 2, NT]), ALU.add).then_inc(sk_ready, 1)

            def normalise(b, g, j):
                h = 16 * b + 2 * g + j
                s = (2 * g + j) % 4
                dve.wait_ge(pv_done, h + 1)
                dve.wait_ge(es_ready, h + 1)
                v4 = vP[:].rearrange("p (c n) -> p c n", c=4)
                dve.tensor_tensor(den[:].unsqueeze(2), v4[:, :, HD:HD + 1], es[:, s, :].unsqueeze(2), ALU.add).then_inc(den_ready, 1)
                dve.wait_ge(den_ready, h + 1)
                dve.reciprocal(rden[:], den[:]).then_inc(rden_ready, 1)
                dve.wait_ge(rden_ready, h + 1)
                if j == 0:
                    wait(dve, ot_done, 8 * b + g - 1)
                dve.tensor_tensor(o_sb[:, g % 2, :, 2 * j:2 * j + 2, :].rearrange("p t a d -> p a t d"),
                                  vP[:].rearrange("p (a t n) -> p a t n", a=2, t=2)[:, :, :, 0:HD],
                                  rden[:].rearrange("p (a t) -> p a t", a=2).unsqueeze(3).broadcast_to([P, 2, NT, HD]),
                                  ALU.mult).then_inc(o_ready, 1)

            def residual(b):
                dve.wait_ge(xb_ready, b)
                dve.wait_ge(out_done, 16 * b)
                wait(dve, x1_stored, 16 * (b - 1))
                for t in range(NT):
                    dve.tensor_tensor(x1[:, t, :], oP[t][:], xb[:, t, :], ALU.add).then_inc(x1_ready, 1)
                dve.wait_ge(x1_ready, 2 * b)
                layernorm_start(x1, st2, mv2, ve2, ln2_chain, 2 * (b - 1), ve2_ready)

            def ln2_end(b):
                dve.wait_ge(rs2_ready, b)
                wait(dve, x1t_done, 2 * (b - 1))
                layernorm_end(x1n, x1, mv2, rs2, x1n_ready)

            dve.wait_ge(c_in, 16 * NCONST)
            dve.wait_ge(ones_set, 1)
            ln1_start(0)
            ln1_end(0)

            def body(b, first=False, last=False, drain=False):
                for g in range(NKV):
                    for j in range(2):
                        gg, jj = (g - 1, 1) if j == 0 else (g, 0)
                        if lagged(b, 0, -gg, first, drain):
                            rotate(b, gg, jj)
                        if lagged(b, g, 3, first, drain):
                            p_evac(b, g - 3, j)
                        if not drain:
                            qkv_evac(b, g, j)
                            cos_part(b, g, j)
                        if lagged(b, g, 2, first, drain):
                            mask_max(b, g - 2, j)
                        gg, jj = (g - 4, 1) if j == 0 else (g - 3, 0)
                        if lagged(b, 0, -gg, first, drain):
                            normalise(b, gg, jj)
                        if g == 5 and j == 0:
                            if not first:
                                residual(b)
                            if not (last or drain):
                                ln1_start(b + 1)
                        if g == 5 and j == 1:
                            if not first:
                                ln2_end(b)
                            if not (last or drain):
                                ln1_end(b + 1)
            batches(dve, body)


def taps_part(nc, ssm, dcoef, pad_dram, factors, fsum):
    with ExitStack() as ctx:
        pad = ctx.enter_context(nc.sbuf_tensor("pad", [CH, PADW], F32))
        dc = ctx.enter_context(nc.sbuf_tensor("dc", [CH, 1], F32))
        fr = ctx.enter_context(nc.sbuf_tensor("fr", [P, 2, KD, D], F32))
        zero_set = ctx.enter_context(nc.semaphore("zero_set"))
        taps_in = ctx.enter_context(nc.semaphore("taps_in"))
        tap0 = ctx.enter_context(nc.semaphore("tap0"))
        pad_out = ctx.enter_context(nc.semaphore("pad_out"))
        f_in = [ctx.enter_context(nc.semaphore(f"f_in{r}")) for r in range(2)]
        f_added = ctx.enter_context(nc.semaphore("f_added"))
        block = ctx.enter_context(nc.Block())

        @block.sync
        def _(sp):
            sp.dma_start(dc[:], dcoef).then_inc(taps_in, 16)
            sp.wait_ge(zero_set, 1)
            sp.dma_start(pad[:, P - 1:P - 1 + D], ssm).then_inc(taps_in, 16)
            sp.dma_start(fsum[:], factors[0]).then_inc(f_in[0], 16)
            for r in range(1, RANK):
                if r > 1:
                    sp.wait_ge(f_added, max(r - 2, 1))
                sp.dma_start(fr[:, r % 2], factors[r]).then_inc(f_in[r % 2], 16)
            sp.wait_ge(tap0, 1)
            sp.dma_start(pad_dram, pad[:]).then_inc(pad_out, 16)
            sp.wait_ge(pad_out, 16)

        @block.vector
        def _(dve):
            dve.memset(pad[:], 0.0).then_inc(zero_set, 1)
            dve.wait_ge(taps_in, 32)
            dve.tensor_tensor(pad[:, P - 1:P], pad[:, P - 1:P], dc[:], ALU.add).then_inc(tap0, 1)
            for r in range(1, RANK):
                dve.wait_ge(f_in[r % 2], 16 * (r // 2 + 1))
                if r == 1:
                    dve.wait_ge(f_in[0], 16)
                if r > 1:
                    dve.wait_ge(f_added, r - 1)
                dve.tensor_tensor(fsum[:], fsum[:], fr[:, r % 2], ALU.add).then_inc(f_added, 1)


def conv_part(nc, ctx_in, pad_dram, q2_dram, big):
    with ExitStack() as ctx:
        def sb(name, shape):
            return ctx.enter_context(nc.sbuf_tensor(name, shape, F32))

        def sem(name):
            return ctx.enter_context(nc.semaphore(name))

        kk = sb("kk", [P, 2, KD, 12, BG])
        tap = sb("tap", [P, 2, D])
        kv = sb("kv", [P, 2, KD, NY])
        qs = sb("qs", [P, 2, KD, 12, BG])
        terms = sb("terms", [P, 2, KD, 8 * 8 * BG])
        res = sb("res", [P, 2, KD, CD * BG])
        y = ctx.enter_context(nc.psum_tensor("y", [P, 2, KD, 512], F32))

        passed2 = sem("passed2")
        q_landed = [sem(f"q_landed{g}") for g in range(NBG)]
        kk_landed = [sem(f"kk_landed{i}") for i in range(2)]
        tap_landed = [sem(f"tap_landed{i}") for i in range(2)]
        kv_ready = sem("kv_ready")
        qs_ready = sem("qs_ready")
        conv_done = sem("conv_done")
        terms_ready = sem("terms_ready")
        res_ready = sem("res_ready")
        res_placed = sem("res_placed")
        block = ctx.enter_context(nc.Block())

        def units(eng, body):
            for bg in range(NBG):
                base = bg * CH
                if bg == 0:
                    body(0, 0, bg, 0)
                    body(1, 1, bg, 1)
                with eng.Fori(1 if bg == 0 else 0, CH // 2) as i:
                    for s in range(2):
                        body(base + 2 * i + s, 2 * i + s, bg, s)

        def wait(eng, s, value):
            if isinstance(value, int) and value <= 0:
                return
            eng.wait_ge(s, value)

        @block.sync
        def _(sp):
            for b in range(B):
                sp.dma_start(big[:, b], q2_dram[b]).then_inc(q_landed[b // BG], 16)

            def body(u, h, bg, s):
                wait(sp, kv_ready, u - 1)
                sp.dma_start(kk[:, s], ctx_in[bg, h]).then_inc(kk_landed[s], 16)
                wait(sp, conv_done, u - 1)
                sp.dma_start(tap[:, s], bass.AP(tensor=pad_dram.tensor, offset=h * PADW, ap=[[1, P], [1, D]]))\
                  .then_inc(tap_landed[s], 16)
            units(sp, body)

        @block.gpsimd
        def _(pool):
            def body(u, h, bg, s):
                pool.wait_ge(kk_landed[s], 8 * (u - s) + 16)
                wait(pool, conv_done, u - 1)
                n = 8 * BG
                k0 = kk[:, s, :, 0:8, :].rearrange("p c i b -> p c (i b)")
                row = k0.ap[1][0]
                shifted = bass.AP(tensor=k0.tensor, offset=k0.offset, ap=[list(k0.ap[0]), [row, KD], [BG, 4], [1, n]])
                pool.tensor_tensor(kv[:, s, :, 0:4 * n].rearrange("p c (d n) -> p c d n", d=4),
                                   k0.unsqueeze(2).broadcast_to([P, KD, 4, n]), shifted, ALU.mult)
                pool.tensor_tensor(kv[:, s, :, 4 * n:NY],
                                   kk[:, s, :, 0:4, :].rearrange("p c i b -> p c (i b)"),
                                   kk[:, s, :, 4:8, :].rearrange("p c i b -> p c (i b)"), ALU.mult).then_inc(kv_ready, 1)
            units(pool, body)

        @block.scalar
        def _(act):
            def fetch(u, h, bg, s):
                wait_apart(act, passed2, (q_landed[bg], 16 * BG), (terms_ready, u - 1))
                mine = big[:, bg * BG:(bg + 1) * BG, :, :]
                act.copy(qs[:, s, :, 0:8, :], mine[:, :, :, bass.ds(h * CD, 8)].rearrange("p b c i -> p c i b"))
                act.copy(qs[:, s, :, 8:12, :], mine[:, :, :, bass.ds(h * CD, 4)].rearrange("p b c i -> p c i b")).then_inc(qs_ready, 1)

            def place(u, h, bg, s):
                wait_apart(act, passed2, (q_landed[bg], 16 * BG), (res_ready, u + 1))
                act.copy(big[:, bg * BG:(bg + 1) * BG, :, bass.ds(h * CD, CD)].rearrange("p b c i -> p c i b"),
                         res[:, s].rearrange("p c (i b) -> p c i b", i=CD)).then_inc(res_placed, 1)

            for bg in range(NBG):
                base = bg * CH
                fetch(base, 0, bg, 0)
                if bg == 0:
                    fetch(1, 1, bg, 1)
                    place(0, 0, bg, 0)
                    fetch(2, 2, bg, 0)
                    place(1, 1, bg, 1)
                with act.Fori(1 if bg == 0 else 0, CH // 2 - 1) as i:
                    for s in range(2):
                        fetch(base + 2 * i + s + 1, 2 * i + s + 1, bg, 1 - s)
                        place(base + 2 * i + s, 2 * i + s, bg, s)
                fetch(base + CH - 1, CH - 1, bg, 1)
                place(base + CH - 2, CH - 2, bg, 0)
                place(base + CH - 1, CH - 1, bg, 1)

        @block.tensor
        def _(pe):
            def body(u, h, bg, s):
                pe.wait_ge(tap_landed[s], 8 * (u - s) + 16)
                pe.wait_ge(kv_ready, u + 1)
                wait(pe, terms_ready, u - 1)
                for d in range(KD):
                    for c in range(d, KD):
                        last = pe.matmul(y[:, s, c, 0:NY], tap[:, s, d * P:(d + 1) * P], kv[:, s, c - d, :],
                                         start=(d == 0), stop=(d == c))
                last.then_inc(conv_done, 1)
            units(pe, body)

        @block.vector
        def _(dve):
            n = CD * BG

            def body(u, h, bg, s):
                dve.wait_ge(qs_ready, u + 1)
                dve.wait_ge(conv_done, u + 1)
                wait(dve, res_ready, u - 1)
                yy = y[:, s, :, 0:NY]
                q0 = qs[:, s, :, 0:8, :].rearrange("p c i b -> p c (i b)")
                tt = terms[:, s]
                part = tt.ap[0]
                row = [8 * n, KD]

                def at(first, *dims):
                    return bass.AP(tensor=tt.tensor, offset=tt.offset + first, ap=[list(part), row, *dims])

                dve.tensor_tensor(at(0, [n + BG, 4], [1, n]), yy[:, :, 0:4 * n].rearrange("p c (d n) -> p c d n", d=4),
                                  q0.unsqueeze(2).broadcast_to([P, KD, 4, n]), ALU.mult)
                dve.tensor_tensor(at(4 * n + 4 * BG, [1, 4 * BG]), yy[:, :, 4 * n:NY], q0[:, :, 0:4 * BG], ALU.mult)
                dve.tensor_tensor(at(n, [n + BG, 4], [1, BG]), yy[:, :, 4 * n:NY].rearrange("p c (a b) -> p c a b", a=4),
                                  qs[:, s, :, 4:8, :], ALU.mult)
                qd = qs[:, s, :, 1:2, :]
                shifted = bass.AP(tensor=qd.tensor, offset=qd.offset, ap=[list(qd.ap[0]), [12 * BG, KD], [BG, 3], [1, n]])
                dve.tensor_tensor(at(5 * n, [n, 3], [1, n]), yy[:, :, n:4 * n].rearrange("p c (d n) -> p c d n", d=3),
                                  shifted, ALU.mult).then_inc(terms_ready, 1)
                dve.wait_ge(terms_ready, u + 1)
                wait(dve, res_placed, u - 1)
                dve.tensor_reduce(res[:, s], at(0, [1, n], [n, 8]), AX.X, ALU.add).then_inc(res_ready, 1)
            units(dve, body)


def mix_part(nc, x1_dram, big, bias, ident, fsum, out):
    NV = B * NT
    with ExitStack() as ctx:
        def sb(name, shape):
            return ctx.enter_context(nc.sbuf_tensor(name, shape, F32))

        def sem(name):
            return ctx.enter_context(nc.semaphore(name))

        def ps(name):
            return [ctx.enter_context(nc.psum_tensor(f"{name}{t}", [P, 512], F32)) for t in range(NT)]

        id3 = sb("id3", [P, P])
        bias3 = sb("bias3", [P, D])
        stage = sb("stage", [P, 2, KD, T])
        xr = sb("xr", [P, 2, NT, D])
        x2 = sb("x2", [P, NT, D])
        x2b = sb("x2b", [P, NT, D])
        xn3 = sb("xn3", [P, NT, D])
        nT = sb("nT", [P, NT, KD, P])
        st3 = sb("st3", [P, NT, 6])
        mv3 = sb("mv3", [P, NT, 2])
        ve3 = sb("ve3", [P, NT])
        rs3 = sb("rs3", [P, NT])
        mhalf3 = sb("mhalf3", [P, NT])
        fin = sb("fin", [P, NT, D])
        aP, nP, fP = ps("aP"), ps("nP"), ps("fP")

        passed3 = sem("passed3")
        const_in = sem("const_in")
        half_set = sem("half_set")
        staged = [sem(f"staged{m}") for m in range(2)]
        xr_landed = [sem(f"xr_landed{m}") for m in range(2)]
        a_done = sem("a_done")
        x2_ready = sem("x2_ready")
        chain3 = sem("chain3")
        ve3_ready = sem("ve3_ready")
        rs3_ready = sem("rs3_ready")
        x2b_ready = sem("x2b_ready")
        xn3_ready = sem("xn3_ready")
        n_done = sem("n_done")
        n_evac = sem("n_evac")
        f_done = sem("f_done")
        fin_ready = sem("fin_ready")
        stored = [sem(f"stored{t}") for t in range(NT)]
        block = ctx.enter_context(nc.Block())

        def wait(eng, s, value):
            if isinstance(value, int) and value <= 0:
                return
            eng.wait_ge(s, value)

        def steps(eng, body, lag=2):
            for v in range(4):
                body(v, v)
            with eng.Fori(1, NV // 4) as i:
                for w in range(4):
                    body(4 * i + w, w)
            for v in range(NV, NV + lag):
                body(v, v % 4)

        def has(v, lag):
            return not isinstance(v, int) or 0 <= v - lag < NV

        @block.sync
        def _(sp):
            sp.dma_start(id3[:], ident).then_inc(const_in, 16)
            sp.dma_start(bias3[:], bias.partition_broadcast(P)).then_inc(const_in, 16)

            def load(v, b, m):
                wait(sp, a_done, v - 2)
                sp.dma_start(stage[:, m], big[:, b]).then_inc(staged[m], 16)
                wait(sp, x2_ready, v - 2)
                sp.dma_start(xr[:, m], x1_dram[b].rearrange("(t p) d -> p t d", p=P)).then_inc(xr_landed[m], 16)

            load(0, 0, 0)
            load(2, 1, 1)
            with sp.Fori(1, NV // 4) as i:
                for m in range(2):
                    load(4 * i + 2 * m, 2 * i + m, m)

        @block.scalar
        def _(act):
            def evac(v, t):
                act.wait_ge(n_done, v + 1)
                wait(act, f_done, v - 1)
                act.copy(nT[:, t], nP[t][:].rearrange("p (c n) -> p c n", c=KD)).then_inc(n_evac, 1)

            def store(v, t, row):
                act.wait_ge(fin_ready, v + 1)
                act.dma_start(row, fin[:, t]).then_inc(stored[t], 16)

            rows = out.rearrange("b (t p) d -> (b t) p d", p=P)

            def body(v, w):
                t = w % 2
                if has(v, 1):
                    evac(v - 1, 1 - t)
                if has(v, 2):
                    store(v - 2, t, rows[v - 2])
            steps(act, body)
            for t in range(NT):
                act.wait_ge(stored[t], 8 * NV)

        @block.gpsimd
        def _(pool):
            pool.memset(mhalf3[:], -0.5).then_inc(half_set, 1)
            pool.wait_ge(half_set, 1)
            pool.wait_ge(const_in, 32)

            def body(v, w):
                t = w % 2
                if has(v, 0):
                    pool.wait_ge(ve3_ready, v + 1)
                    pool.tensor_tensor(rs3[:, t:t + 1], ve3[:, t:t + 1], mhalf3[:, t:t + 1], ALU.pow).then_inc(rs3_ready, 1)
                    wait(pool, fin_ready, v - 1)
                    pool.tensor_tensor(x2b[:, t], x2[:, t], bias3[:], ALU.add).then_inc(x2b_ready, 1)
            steps(pool, body, lag=0)

        @block.tensor
        def _(pe):
            pe.wait_ge(const_in, 32)

            def body(v, w):
                t, m = w % 2, w // 2
                if has(v, 0):
                    pe.wait_ge(staged[m], 4 * (v - w) + 16)
                    wait(pe, x2_ready, v - 1)
                    for c in range(KD):
                        last = pe.transpose(aP[t][:, c * P:(c + 1) * P], stage[:, m, c, t * P:(t + 1) * P], id3[:])
                    last.then_inc(a_done, 1)
                if has(v, 1):
                    pe.wait_ge(xn3_ready, v)
                    wait(pe, n_evac, v - 2)
                    for c in range(KD):
                        last = pe.transpose(nP[1 - t][:, c * P:(c + 1) * P], xn3[:, 1 - t, c * P:(c + 1) * P], id3[:])
                    last.then_inc(n_done, 1)
                if has(v, 2):
                    pe.wait_ge(n_evac, v - 1)
                    wait(pe, fin_ready, v - 3)
                    for c in range(KD):
                        last = pe.matmul(fP[t][:], nT[:, t, c, :], fsum[:, c, :], start=(c == 0), stop=(c == KD - 1))
                    last.then_inc(f_done, 1)
            steps(pe, body)

        @block.vector
        def _(dve):
            dve.wait_ge(const_in, 32)

            def body(v, w):
                t, m = w % 2, w // 2
                if has(v, 0):
                    dve.wait_ge(xr_landed[m], 4 * (v - w) + 16)
                    dve.wait_ge(a_done, v + 1)
                    wait(dve, x2b_ready, v - 1)
                    dve.tensor_tensor(x2[:, t], aP[t][:], xr[:, m, t], ALU.add).then_inc(x2_ready, 1)
                    dve.wait_ge(x2_ready, v + 1)
                    dve.bn_stats(st3[:, t], x2[:, t]).then_inc(chain3, 1)
                    wait_apart(dve, passed3, (chain3, 2 * v + 1))
                    dve.bn_aggr(mv3[:, t], st3[:, t]).then_inc(chain3, 1)
                    dve.wait_ge(chain3, 2 * v + 2)
                    dve.tensor_scalar(ve3[:, t:t + 1], mv3[:, t, 1:2], EPS, None, ALU.add).then_inc(ve3_ready, 1)
                if has(v, 2):
                    dve.wait_ge(f_done, v - 1)
                    dve.wait_ge(x2b_ready, v - 1)
                    wait(dve, stored[t], 8 * (v - t) - 16)
                    dve.scalar_tensor_tensor(fin[:, t], fP[t][:], 1.0 / math.sqrt(RANK), x2b[:, t], ALU.mult, ALU.add)                       .then_inc(fin_ready, 1)
                if has(v, 0):
                    dve.wait_ge(rs3_ready, v + 1)
                    wait(dve, n_done, v - 1)
                    dve.tensor_scalar(xn3[:, t], x2[:, t], mv3[:, t, 0:1], rs3[:, t:t + 1],
                                      ALU.subtract, ALU.mult).then_inc(xn3_ready, 1)
            steps(dve, body)


def decoder_layer(nc, x, ctxt, wqkv, bqkv, wout, bout, sinks, ssm, dcoef, factors, bias, rope, masks, ident, out):
    x1_dram = nc.dram_tensor("x1_rows", [B, T, D], F32).ap()
    q2_dram = nc.dram_tensor("q2_cols", [B, P, KD, T], F32).ap()
    pad_dram = nc.dram_tensor("padded_taps", [CH, PADW], F32).ap()
    with nc.sbuf_tensor("fsum", [P, KD, D], F32) as fsum:
        taps_part(nc, ssm, dcoef, pad_dram, factors, fsum)
        attention_part(nc, x, wqkv, bqkv, wout, bout, sinks, rope, masks, ident, x1_dram, q2_dram)
        with nc.sbuf_tensor("big", [P, B, KD, T], F32) as big:
            conv_part(nc, ctxt, pad_dram, q2_dram, big)
            mix_part(nc, x1_dram, big, bias, ident, fsum, out)



def layout(inputs):
    a = {k: np.asarray(v) for k, v in inputs.items()}
    wq, bq = a["L0_attn_qkv_w"], a["L0_attn_qkv_b"]
    nq, nk = NH * HD, NKV * HD
    w = np.concatenate([wq[:nq].reshape(NKV, QM * HD, D), wq[nq:nq + nk].reshape(NKV, HD, D),
                        wq[nq + nk:].reshape(NKV, HD, D)], axis=1)
    bias = np.concatenate([bq[:nq].reshape(NKV, QM * HD), bq[nq:nq + nk].reshape(NKV, HD),
                           bq[nq + nk:].reshape(NKV, HD)], axis=1)
    c = a["ctx_2048"].reshape(NBG, BG, CH, CD, KD, P)[..., ::-1].transpose(0, 2, 5, 4, 3, 1)
    c = np.concatenate([c, c[:, :, :, :, 0:4]], axis=4)
    return {
        "x": a["x"],
        "ctxt": np.ascontiguousarray(c),
        "ssm": a["L0_xattn_ssm_kernel"],
        "dcoef": a["L0_xattn_D"].reshape(CH, 1),
        "factors": np.ascontiguousarray(a["L0_ffn_factors"].reshape(RANK, KD, P, D).transpose(0, 2, 1, 3)),
        "bias": a["L0_ffn_bias"],
        "wqkv": np.ascontiguousarray(w.reshape(NKV, GW, KD, P).transpose(3, 2, 0, 1)),
        "bqkv": np.ascontiguousarray(bias.reshape(-1)),
        "wout": np.ascontiguousarray(a["L0_attn_out_w"].reshape(D, NH * HD // P, P).transpose(2, 1, 0)),
        "bout": a["L0_attn_out_b"],
        "sinks": a["L0_attn_sinks"],
        "rope": rope_tables(),
        "masks": score_masks(),
        "ident": np.eye(P, dtype=np.float32),
    }


def kernel(**inputs):
    import concourse.bacc as bacc
    from concourse.bass_utils import run_bass_kernel_spmd

    nc = bacc.Bacc("TRN2", target_bir_lowering=False, num_devices=1)
    arrays = layout(inputs)
    args = {name: nc.dram_tensor(f"in_{name}", a.shape, mybir.dt.from_np(a.dtype), kind="ExternalInput").ap()
            for name, a in arrays.items()}
    out = nc.dram_tensor("out_rows", [B, T, D], F32, kind="ExternalOutput").ap()
    decoder_layer(nc, out=out, **args)
    r = run_bass_kernel_spmd(nc, [{f"in_{name}": a for name, a in arrays.items()}], core_ids=[0])
    return r.results[0]["out_rows"]
```

```python
import math
from contextlib import ExitStack

import numpy as np

import concourse.bass as bass
from concourse import mybir

F32 = mybir.dt.float32
F32R = mybir.dt.float32r
ALU = mybir.AluOpType
ACT = mybir.ActivationFunctionType
AX = mybir.AxisListType

P = 128
B, T, D = 16, 256, 512
NT = T // P
KD = D // P
HD = 64
NKV, QM = 8, 4
NH = NKV * QM
GS = NKV // 2
GW = (QM + 2) * HD
RW = (QM + 1) * HD
SM_SCALE = 1.0 / math.sqrt(HD)
MASKED = -1.0e30
CHUNK = 2 * (QM + 2) * HD
EPS = 1e-5
SK = P + T

CH, CD = 32, 8
RANK = 8
NPAIR = CD * (CD + 1) // 2
BG = 8
NBG = B // BG
NY = BG * NPAIR
PADW = P + D


def rope_tables():
    theta, scaling, alpha, beta, icl = 150000.0, 32.0, 1.0, 32.0, 256
    half = HD // 2
    freq = theta ** (np.arange(0, HD, 2, dtype=np.float32) / HD)
    conc = 0.1 * math.log(scaling) + 1.0
    low = half * math.log(icl / (beta * 2 * math.pi)) / math.log(theta)
    high = half * math.log(icl / (alpha * 2 * math.pi)) / math.log(theta)
    ramp = np.clip((np.arange(half, dtype=np.float32) - low) / (high - low), 0.0, 1.0)
    mask = 1.0 - ramp
    inv = 1.0 / (scaling * freq) * (1.0 - mask) + 1.0 / freq * mask
    ang = np.outer(np.arange(T, dtype=np.float32), inv)
    cos = (np.cos(ang) * conc).astype(np.float32)
    sin = (np.sin(ang) * conc).astype(np.float32)
    tab = np.concatenate([cos, cos, -sin, sin], axis=1).reshape(NT, P, 2 * HD)
    return np.ascontiguousarray(tab.transpose(1, 0, 2))


def score_masks():
    q, k = np.arange(P)[:, None], np.arange(P)[None, :]
    same = np.where(k > q, MASKED, 0.0)
    before = np.where(k <= q, MASKED, 0.0)
    return np.concatenate([same, before, same], axis=1).astype(np.float32)


def wait_apart(eng, passed, *waits):
    for s, v in waits:
        if not isinstance(v, int) or v > 0:
            eng.wait_ge(s, v)
    eng.sem_inc(passed, 1)


def attention_part(nc, x, wqkv, bqkv, wout, bout, sinks, rope, masks, ident, factors, ssm_pad, dcoef,
                   x1_dram, q2_dram, pad_dram, fsum):
    part_dram = nc.dram_tensor("x_part_rows", [B, T, D], F32).ap()
    wq_dram = nc.dram_tensor("w_split", [GS, 2, P, KD * GW], F32).ap()
    wo_dram = nc.dram_tensor("wo_split", [GS, 2, P, 2 * D], F32).ap()
    with ExitStack() as ctx:
        def sb(name, shape, dt=F32):
            return ctx.enter_context(nc.sbuf_tensor(name, shape, dt))

        def ps(name):
            return ctx.enter_context(nc.psum_tensor(name, [P, 512], F32))

        def sem(name):
            return ctx.enter_context(nc.semaphore(name))

        wh = sb("wh", [P, GS, KD, GW], F32R)
        wl = sb("wl", [P, GS, KD, GW], F32R)
        woh = sb("woh", [P, GS, 2, D], F32R)
        wol = sb("wol", [P, GS, 2, D], F32R)
        bias_sb = sb("bias_sb", [P, GS, GW])
        bo_sb = sb("bo_sb", [P, D])
        sink_sb = sb("sink_sb", [P, NH])
        rope_sb = sb("rope_sb", [P, NT, 2, HD])
        mask_sb = sb("mask_sb", [P, SK])
        id_sb = sb("id_sb", [P, P])
        x_in = sb("x_in", [P, NT, D])
        xn = sb("xn", [P, NT, D])
        xTh = sb("xTh", [P, 2, NT, KD, P], F32R)
        xTl = sb("xTl", [P, 2, NT, KD, P], F32R)
        stats = sb("stats", [P, NT, 6])
        mv = sb("mv", [P, NT, 2])
        veps = sb("veps", [P, NT])
        rstd = sb("rstd", [P, NT])
        mhalf = sb("mhalf", [P, NT])
        qk = sb("qk", [P, 2, QM + 1, HD])
        m1 = sb("m1", [P, 2, QM + 1, HD])
        m2 = sb("m2", [P, 2, QM + 1, HD])
        qr = sb("qr", [P, 2, QM + 2, HD])
        vv = sb("vv", [P, NKV, NT, HD + 1])
        qTh = sb("qTh", [P, 2, 3, T], F32R)
        qTl = sb("qTl", [P, 2, 3, T], F32R)
        pr = sb("pr", [P, 4, 2, SK])
        mx = sb("mx", [P, 4, 2 * NT])
        nm = sb("nm", [P, 4, 2 * NT])
        sk = sb("sk", [P, 4, 2 * NT])
        es = sb("es", [P, 4, 2 * NT])
        pT = sb("pT", [P, 2, 2, SK])
        den = sb("den", [P, 2 * NT])
        rden = sb("rden", [P, 2 * NT])
        o_sb = sb("o_sb", [P, 2, NT, QM, HD])
        oTh = sb("oTh", [P, 2, NT, 2, P], F32R)
        oTl = sb("oTl", [P, 2, NT, 2, P], F32R)
        xb = sb("xb", [P, NT, D])
        x1 = sb("x1", [P, NT, D])
        work = sb("work", [P, 3 * CHUNK])
        x1n = work[:, 0:NT * D].rearrange("p (t d) -> p t d", t=NT)
        x1T = work[:, NT * D:2 * NT * D].rearrange("p (c t) -> p c t", c=KD)
        st2 = sb("st2", [P, NT, 6])
        mv2 = sb("mv2", [P, NT, 2])
        ve2 = sb("ve2", [P, NT])
        rs2 = sb("rs2", [P, NT])
        tap0 = sb("tap0", [CH, 2])

        wP = ps("wP")
        tP = ps("tP")
        sP = [ps("sP0"), ps("sP1")]
        pP = ps("pP")
        vP = ps("vP")
        oP = [ps("oP0"), ps("oP1")]

        c_in = sem("c_in")
        id_in = sem("id_in")
        mask_landed = sem("mask_landed")
        passed = sem("passed")
        raw_in = [sem(f"raw_in{i}") for i in range(3)]
        hi_done = sem("hi_done")
        lo_done = sem("lo_done")
        spill = sem("spill")
        w_in = [sem(f"w_in{g}") for g in range(GS)]
        wo_in = [sem(f"wo_in{g}") for g in range(GS)]
        tap_in = sem("tap_in")
        tap_added = sem("tap_added")
        tap_out = sem("tap_out")
        f_in = sem("f_in")
        x_landed = sem("x_landed")
        xb_landed = sem("xb_landed")
        mhalf_set = sem("mhalf_set")
        ones_set = sem("ones_set")
        ln_chain = sem("ln_chain")
        ve_ready = sem("ve_ready")
        rstd_ready = sem("rstd_ready")
        xn_ready = sem("xn_ready")
        xt_done = sem("xt_done")
        xt_hi = sem("xt_hi")
        xt_lo = sem("xt_lo")
        qkv_done = sem("qkv_done")
        qk_ready = sem("qk_ready")
        v_ready = sem("v_ready")
        m_ready = sem("m_ready")
        qr_ready = sem("qr_ready")
        qt_done = sem("qt_done")
        qt_hi = sem("qt_hi")
        qt_lo = sem("qt_lo")
        s_done = sem("s_done")
        masked = sem("masked")
        nm_ready = sem("nm_ready")
        sk_ready = sem("sk_ready")
        exp_done = sem("exp_done")
        es_ready = sem("es_ready")
        pt_done = sem("pt_done")
        pt_evac = sem("pt_evac")
        pv_done = sem("pv_done")
        den_ready = sem("den_ready")
        rden_ready = sem("rden_ready")
        o_ready = sem("o_ready")
        ot_done = sem("ot_done")
        ot_hi = sem("ot_hi")
        ot_lo = sem("ot_lo")
        out_done = sem("out_done")
        xb_ready = sem("xb_ready")
        x1_ready = sem("x1_ready")
        ln2_chain = sem("ln2_chain")
        ve2_ready = sem("ve2_ready")
        rs2_ready = sem("rs2_ready")
        x1n_ready = sem("x1n_ready")
        x1t_done = sem("x1t_done")
        x1t_evac = sem("x1t_evac")
        x1_stored = sem("x1_stored")
        x1t_stored = sem("x1t_stored")

        block = ctx.enter_context(nc.Block())
        NCONST = 4
        NM, HM = 2 * B // 2, B // 2

        def chunks(gs):
            return [("qkv", g, i) for g in gs for i in range(2)] + [("out", g, i) for g in gs for i in range(2)]

        first_chunks, second_chunks = chunks(range(GS)), chunks(range(GS, NKV))
        NF = len(first_chunks)

        def raw_of(c):
            kind, g, i = c
            if kind == "qkv":
                return wqkv[:, i * 2:i * 2 + 2, g, :], 2 * GW
            return wout[:, 2 * g + i, :], D

        def placed(c, w, wo):
            kind, g, i = c
            if kind == "qkv":
                return w[:, g % GS, i * 2:i * 2 + 2, :].rearrange("p c n -> p (c n)")
            return wo[:, g % GS, i, :]

        FIRST_PEELED = 4

        def first_of(k):
            return range(min(FIRST_PEELED + 2 * k, NF), min(FIRST_PEELED + 2 * k + 2, NF))

        def second_step(n):
            return divmod((NF - FIRST_PEELED) // 2 + n, 16)

        def second_of(number, k):
            return [n for n in range(len(second_chunks)) if second_step(n) == (number, k)]

        def wait(eng, s, value):
            if isinstance(value, int) and value <= 0:
                return
            eng.wait_ge(s, value)

        class Body:

            def __init__(self, m, sweep, number=None):
                self.m, self.sweep, self.number = m, sweep, number
                self.first = number == 0
                self.drain = number == NM
                self.joint = number == HM

            def here(self, p, lag):
                n = p - lag
                return not (self.first and n < 0) and not (self.drain and n >= 0)

            def old_sweep(self):
                return 0 if self.joint else self.sweep

        def bodies(eng, body):
            body(Body(0, 0, 0))
            body(Body(1, 0, 1))
            with eng.Fori(2, HM - 1) as m:
                body(Body(m, 0))
            body(Body(HM - 1, 0, HM - 1))
            body(Body(HM, 1, HM))
            body(Body(HM + 1, 1, HM + 1))
            with eng.Fori(HM + 2, NM - 1) as m:
                body(Body(m, 1))
            body(Body(NM - 1, 1, NM - 1))
            body(Body(NM, 1, NM))

        def x_next(y, p, j):
            return p % 4 in (1, 2) and j == 0 and not (y.drain or y.number == NM - 1 and p >= 4)

        def rows(a, b):
            return a[b].rearrange("(t p) d -> p t d", p=P)

        @block.sync
        def _(sp):
            sp.dma_start(x_in[:], rows(x, 0)).then_inc(x_landed, 16)
            sp.dma_start(id_sb[:], ident).then_inc(id_in, 16)

            def load_raw(n, c):
                src, width = raw_of(c)
                dst = work[:, (n % 3) * CHUNK:(n % 3) * CHUNK + width]
                if c[0] == "qkv":
                    dst = dst.rearrange("p (c n) -> p c n", c=2)
                sp.dma_start(dst, src).then_inc(raw_in[n % 3], 16)

            for n, c in enumerate(first_chunks):
                if n == 2:
                    sp.dma_start(bias_sb[:].rearrange("p g n -> p (g n)"), bqkv[0:GS * GW].partition_broadcast(P)).then_inc(c_in, 16)
                    sp.dma_start(rope_sb[:].rearrange("p t a d -> p t (a d)"), rope).then_inc(c_in, 16)
                if n == 4:
                    sp.dma_start(mask_sb[:], masks).then_inc(mask_landed, 16)
                    sp.dma_start(sink_sb[:], sinks.partition_broadcast(P)).then_inc(c_in, 16)
                    sp.dma_start(bo_sb[:], bout.partition_broadcast(P)).then_inc(c_in, 16)
                if n == 6:
                    sp.wait_ge(xn_ready, 2)
                    sp.dma_start(x_in[:], rows(x, 1)).then_inc(x_landed, 16)
                if n >= 3:
                    sp.wait_ge(lo_done, n - 2)
                load_raw(n, c)
            sp.dma_start(tap0[:, 0:1], ssm_pad[:, P - 1:P], allow_slow_non_contiguous=True).then_inc(tap_in, 16)
            sp.dma_start(tap0[:, 1:2], dcoef).then_inc(tap_in, 16)
            sp.dma_start(pad_dram, ssm_pad).then_inc(tap_in, 16)
            sp.dma_start(xb[:], rows(x, 0)).then_inc(xb_landed, 16)

            def split_loads(n):
                sp.wait_ge(lo_done, NF + n)
                load_raw(3 * (NF + n), second_chunks[n])

            def split_stores(n):
                kind, g, i = second_chunks[n]
                width = raw_of(second_chunks[n])[1]
                dst = (wq_dram if kind == "qkv" else wo_dram)[g - GS]
                sp.wait_ge(hi_done, NF + n + 1)
                sp.wait_ge(lo_done, NF + n + 1)
                for part in range(2):
                    sp.dma_start(dst[part][:, i * width:(i + 1) * width],
                                 work[:, (part + 1) * CHUNK:(part + 1) * CHUNK + width]).then_inc(spill, 16)

            def body(y):
                m = y.m
                if y.first:
                    sp.wait_ge(xn_ready, 4)
                    sp.dma_start(x_in[:], rows(x, 2)).then_inc(x_landed, 16)
                for n in range(len(second_chunks)):
                    if y.number == second_step(n)[0]:
                        split_loads(n)
                        split_stores(n)
                if y.first:
                    sp.wait_ge(xn_ready, 6)
                    sp.dma_start(x_in[:], rows(x, 3)).then_inc(x_landed, 16)
                    return
                if y.number == 1:
                    sp.wait_ge(tap_added, 1)
                    sp.wait_ge(tap_in, 48)
                    sp.dma_start(pad_dram[:, P - 1:P], tap0[:, 0:1], allow_slow_non_contiguous=True).then_inc(tap_out, 16)
                for a in range(2):
                    b = 2 * m + a + 1 - B * y.sweep
                    if y.number == HM - 1 and a == 1:
                        b = 0
                    if not (y.drain or y.number == NM - 1 and a == 1 or y.number == 1 and a == 0):
                        sp.wait_ge(xn_ready, 4 * m + 2 * a + 2)
                        sp.dma_start(x_in[:], rows(x, b)).then_inc(x_landed, 16)
                    b = 2 * m - 2 + a - B * y.old_sweep()
                    sp.wait_ge(x1_ready, 4 * m - 2 + 2 * a)
                    sp.dma_start(rows(x1_dram if y.old_sweep() else part_dram, b), x1[:]).then_inc(x1_stored, 16)
                    if not (y.drain and a == 1):
                        nb = b + 1
                        late = y.old_sweep() == 1
                        if y.joint and a == 1:
                            nb, late = 0, True
                        if late:
                            sp.wait_ge(x1_stored, 16 * (2 * m - B + a))
                        sp.dma_start(xb[:], rows(part_dram if late else x, nb)).then_inc(xb_landed, 16)
                    if y.old_sweep():
                        sp.wait_ge(x1t_evac, 4 * m - 2 + 2 * a - 2 * B)
                        sp.dma_start(q2_dram[b], x1T).then_inc(x1t_stored, 16)
            bodies(sp, body)
            sp.wait_ge(x1_stored, 16 * 2 * B)
            sp.wait_ge(x1t_stored, 16 * B)
            sp.wait_ge(tap_out, 16)

        @block.tensor
        def _(pe):
            pe.wait_ge(id_in, 16)

            def tp_free(y, p, j, slot):
                w = 2 * y.m + p // 4
                r = p % 4
                last = slot == "last"
                q_uses = 16 * NM if y.drain and p > 0 else 16 * y.m + 2 * (p - 1) + j + last
                o_uses = 8 * NM if y.drain and p >= 4 else 8 * y.m + p - 4
                x_uses = 2 * (w + 1) + int((r, j) > (1, 0)) + int((r, j) > (2, 0))
                if y.drain or y.number == NM - 1 and p >= 4:
                    x_uses = 4 * B
                x1_uses = 2 * (w - 2 - B) + (0 if r < 3 or j == 0 else 1 if slot == "first" else 2)
                if y.first or y.drain or y.joint or y.number == NM - 1:
                    wait(pe, qt_lo, q_uses)
                    wait(pe, ot_lo, o_uses)
                    wait(pe, xt_lo, x_uses)
                    if y.old_sweep():
                        wait(pe, x1t_evac, x1_uses)
                elif slot == "last":
                    pe.wait_ge(qt_lo, q_uses)
                elif slot == "first":
                    pe.wait_ge(x1t_evac, x1_uses)
                elif j == 0:
                    pe.wait_ge(ot_lo, o_uses)
                elif r in (1, 2):
                    pe.wait_ge(xt_lo, x_uses)
                elif r == 3 and y.old_sweep():
                    pe.wait_ge(x1t_evac, x1_uses)
                else:
                    pe.wait_ge(qt_lo, q_uses)

            def x_transposes(v, j):
                pe.wait_ge(xn_ready, 2 * v + j + 1)
                for c in range(KD):
                    last = pe.transpose(tP[:, c * P:(c + 1) * P], xn[:, j, c * P:(c + 1) * P], id_sb[:])
                last.then_inc(xt_done, 1)

            def qkv(y, p, j):
                h = 16 * y.m + 2 * p + j
                v = 2 * y.m + p // 4
                g = p % GS
                if p % 4 == 0:
                    pe.wait_ge(xt_lo, 2 * v + j + 1)
                if y.first and p < GS:
                    pe.wait_ge(lo_done, 2 * p + 2)
                if y.joint and p < GS:
                    pe.wait_ge(w_in[p], 48)
                wait(pe, qk_ready, h)
                wait(pe, v_ready, h)
                steps = [(xTh, wh), (xTl, wh), (xTh, wl)]
                for c in range(KD):
                    for n, (a, w) in enumerate(steps):
                        last = pe.matmul(wP[:, 0:GW], a[:, p // 4, j, c, :], w[:, g, c, :],
                                         start=(c == 0 and n == 0), stop=(c == KD - 1 and n == 2))
                last.then_inc(qkv_done, 1)

            def q_transposes(y, p, j):
                h = 16 * y.m + 2 * (p - 1) + j
                pe.wait_ge(qr_ready, h + 1)
                tp_free(y, p, j, "middle")
                for c in range(3):
                    last = pe.transpose(tP[:, c * P:(c + 1) * P],
                                        qr[:, j, 2 * c:2 * c + 2, :].rearrange("p a d -> p (a d)"), id_sb[:])
                last.then_inc(qt_done, 1)

            def scores(y, p, j):
                h = 16 * y.m + 2 * (p - 2) + j
                s = p % 2
                pe.wait_ge(qt_lo, h - j + 2)
                wait(pe, masked, h)
                for t in range(NT):
                    for a in range(2):
                        r = slice(a * HD, a * HD + HD)
                        k0 = t * P
                        for n, (q, k) in enumerate([(qTh, qTh), (qTl, qTh), (qTh, qTl)]):
                            last = pe.matmul(sP[a][:, k0:P + 2 * k0], q[r, s, j, t * P:(t + 1) * P],
                                             k[r, s, 2, 0:(t + 1) * P], start=(n == 0), stop=(n == 2))
                last.then_inc(s_done, 1)

            def p_transposes(y, p, j, a):
                h = 16 * y.m + 2 * (p - 3) + j
                pe.wait_ge(exp_done, 2 * h + a + 1)
                wait(pe, pt_evac, 2 * h + a)
                for c in range(3):
                    last = pe.transpose(pP[:, c * P:(c + 1) * P], pr[:, (2 * p + 2 + j) % 4, a, c * P:(c + 1) * P], id_sb[:])
                last.then_inc(pt_done, 1)

            def pv(y, u, j):
                h = 16 * y.m + 2 * u + j
                s = j % 2
                vu = vv[:, u % NKV]
                pe.wait_ge(pt_evac, 2 * h + 2)
                pe.wait_ge(v_ready, h - j + 2)
                pe.wait_ge(ones_set, 1)
                wait(pe, o_ready, h)
                for a in range(2):
                    o = vP[:, a * P * 2:a * P * 2 + HD + 1]
                    pe.matmul(o, pT[:, s, a, 0:P], vu[:, 0, :], start=True, stop=True)
                    o = vP[:, a * P * 2 + P:a * P * 2 + P + HD + 1]
                    pe.matmul(o, pT[:, s, a, P:2 * P], vu[:, 0, :], start=True, stop=False)
                    last = pe.matmul(o, pT[:, s, a, 2 * P:3 * P], vu[:, 1, :], start=False, stop=True)
                last.then_inc(pv_done, 1)

            def o_transposes(y, p):
                u = 8 * y.m + p - 4
                pe.wait_ge(o_ready, 2 * u + 2)
                tp_free(y, p, 1, "last")
                for t in range(NT):
                    for c in range(2):
                        last = pe.transpose(tP[:, (2 * t + c) * P:(2 * t + c + 1) * P],
                                            o_sb[:, p % 2, t, 2 * c:2 * c + 2, :].rearrange("p a d -> p (a d)"), id_sb[:])
                last.then_inc(ot_done, 1)

            def out_projection(y, p, j):
                u = 8 * y.m + p - 5
                g = (p - 5) % GS
                pe.wait_ge(ot_lo, u + 1)
                if y.first:
                    pe.wait_ge(lo_done, 2 * GS + 2 * (p - 5) + 2)
                if y.number == 1 and p == 0:
                    pe.wait_ge(lo_done, NF)
                if y.joint and p >= 5:
                    pe.wait_ge(wo_in[g], 32)
                if y.number == HM + 1 and p == 0:
                    pe.wait_ge(wo_in[g], 32)
                if g == 0:
                    wait(pe, x1_ready, 4 * y.m + 2 * ((p - 5) // 4) - 1 + j)
                steps = [(oTh, woh), (oTl, woh), (oTh, wol)]
                for c in range(2):
                    for n, (a, w) in enumerate(steps):
                        last = pe.matmul(oP[j][:], a[:, (p - 5) % 2, j, c, :], w[:, g, c, :],
                                         start=(g == 0 and c == 0 and n == 0), stop=(g == GS - 1 and c == 1 and n == 2))
                last.then_inc(out_done, 1)

            def x1_transposes(y, p, j):
                pe.wait_ge(x1n_ready, 4 * y.m - 4 + 2 * (p // 4) - 2 * B + j + 1)
                tp_free(y, p, j, "first" if j else "last")
                for c in range(KD):
                    last = pe.transpose(tP[:, c * P:(c + 1) * P], x1n[:, j, c * P:(c + 1) * P], id_sb[:])
                last.then_inc(x1t_done, 1)

            x_transposes(0, 0)
            pe.wait_ge(xt_lo, 1)
            x_transposes(0, 1)

            def body(y):
                for p in range(8):
                    for j in range(2):
                        if y.here(p, 3):
                            p_transposes(y, p, j, 0)
                        if not y.drain:
                            qkv(y, p, j)
                        if p % 4 == 3 and j == 1 and y.old_sweep():
                            x1_transposes(y, p, j)
                        if y.here(p, 3):
                            p_transposes(y, p, j, 1)
                        if y.here(p, 1):
                            q_transposes(y, p, j)
                        if y.here(p, 2):
                            scores(y, p, j)
                        if x_next(y, p, j):
                            tp_free(y, p, j, "last")
                            x_transposes(2 * y.m + p // 4 + 1, p % 4 - 1)
                        if p % 4 == 3 and j == 0 and y.old_sweep():
                            x1_transposes(y, p, j)
                        if j == 1 and y.here(p, 4):
                            o_transposes(y, p)
                        u, jj = (p - 4, 1) if j == 0 else (p - 3, 0)
                        if y.here(u, 0):
                            pv(y, u, jj)
                        if y.here(p, 5):
                            out_projection(y, p, j)
            bodies(pe, body)

        @block.scalar
        def _(act):
            def split_high(n, src, dst):
                act.copy(dst, src).then_inc(hi_done, 1)

            def second_high(n):
                width = raw_of(second_chunks[n])[1]
                act.wait_ge(raw_in[0], 16 * ((NF + 2) // 3 + n + 1))
                wait(act, spill, 32 * n)
                if n == 0:
                    act.wait_ge(lo_done, NF)
                split_high(n, work[:, 0:width], work[:, CHUNK:CHUNK + width].bitcast(F32R))

            def reload(g):
                act.wait_ge(qkv_done, 16 * (HM - 1) + 2 * (4 + g) + 2)
                act.wait_ge(v_ready, 16 * (HM - 1) + 2 * (4 + g) + 2)
                act.wait_ge(spill, 32 * len(second_chunks))
                act.dma_start(wh[:, g].rearrange("p c n -> p (c n)").bitcast(F32), wq_dram[g, 0]).then_inc(w_in[g], 16)
                act.dma_start(wl[:, g].rearrange("p c n -> p (c n)").bitcast(F32), wq_dram[g, 1]).then_inc(w_in[g], 16)
                act.dma_start(bias_sb[:, g], bqkv[(GS + g) * GW:(GS + g + 1) * GW].partition_broadcast(P)).then_inc(w_in[g], 16)

            def reload_out(g):
                act.wait_ge(out_done, 16 * (HM - 1) + 2 * (4 + g) + 2)
                act.dma_start(woh[:, g].rearrange("p c n -> p (c n)").bitcast(F32), wo_dram[g, 0]).then_inc(wo_in[g], 16)
                act.dma_start(wol[:, g].rearrange("p c n -> p (c n)").bitcast(F32), wo_dram[g, 1]).then_inc(wo_in[g], 16)

            def x_high(v, s, j):
                act.wait_ge(xt_done, 2 * v + j + 1)
                wait(act, qkv_done, 8 * v - 8)
                act.copy(xTh[:, s, j], tP[:, 0:D].rearrange("p (c t) -> p c t", c=KD)).then_inc(xt_hi, 1)

            def q_evac(y, p, j):
                h = 16 * y.m + 2 * (p - 1) + j
                act.wait_ge(qt_done, h + 1)
                wait(act, s_done, h - j - 2)
                act.copy(qTh[:, (p - 1) % 2, :, j * P:(j + 1) * P],
                         tP[:, 0:3 * P].rearrange("p (c t) -> p c t", c=3)).then_inc(qt_hi, 1)

            def exps(y, p, j):
                h = 16 * y.m + 2 * (p - 2) + j
                s = (2 * p + j) % 4
                act.wait_ge(nm_ready, h + 1)
                for a in range(2):
                    for t in range(NT):
                        cols = slice(t * P, P + 2 * t * P)
                        last = act.activation(pr[:, s, a, cols], pr[:, s, a, cols], ACT.Exp,
                                              bias=nm[:, s, 2 * a + t:2 * a + t + 1], scale=SM_SCALE)
                    last.then_inc(exp_done, 1)
                act.wait_ge(sk_ready, h + 1)
                wait(act, den_ready, h - 3)
                act.activation(es[:, s, :], sk[:, s, :], ACT.Exp).then_inc(es_ready, 1)

            def p_evac(y, p, j, a):
                h = 16 * y.m + 2 * (p - 3) + j
                act.wait_ge(pt_done, 2 * h + a + 1)
                if a == 0:
                    wait(act, pv_done, h - 1)
                act.copy(pT[:, j, a, :], pP[:, 0:SK]).then_inc(pt_evac, 1)

            def o_high(y, p):
                u = 8 * y.m + p - 4
                act.wait_ge(ot_done, u + 1)
                wait(act, out_done, 2 * u - 2)
                act.copy(oTh[:, p % 2].rearrange("p t c n -> p (t c n)"), tP[:, 0:512]).then_inc(ot_hi, 1)

            def x1_evac(y, p, j):
                n = 4 * y.m - 4 + 2 * (p // 4) - 2 * B + j
                act.wait_ge(x1t_done, n + 1)
                wait(act, x1t_stored, 8 * (n - j))
                act.copy(x1T[:, :, j * P:(j + 1) * P], tP[:, 0:D].rearrange("p (c t) -> p c t", c=KD)).then_inc(x1t_evac, 1)

            def first_high(n):
                width = raw_of(first_chunks[n])[1]
                act.wait_ge(raw_in[n % 3], 16 * (n // 3 + 1))
                split_high(n, work[:, (n % 3) * CHUNK:(n % 3) * CHUNK + width], placed(first_chunks[n], wh, woh))

            for n in range(FIRST_PEELED):
                first_high(n)
                if n < NT:
                    x_high(0, 0, n)

            def body(y):
                for p in range(8):
                    for j in range(2):
                        if y.here(p, 3):
                            p_evac(y, p, j, 0)
                        if p % 4 == 3 and j == 1 and y.old_sweep():
                            x1_evac(y, p, j)
                        if y.here(p, 3):
                            p_evac(y, p, j, 1)
                        if y.here(p, 1):
                            q_evac(y, p, j)
                        if x_next(y, p, j):
                            x_high(2 * y.m + p // 4 + 1, (p // 4 + 1) % 2, p % 4 - 1)
                        if p % 4 == 3 and j == 0 and y.old_sweep():
                            x1_evac(y, p, j)
                        if j == 1 and y.here(p, 4):
                            o_high(y, p)
                        if y.here(p, 2):
                            exps(y, p, j)
                        if y.first:
                            for n in first_of(2 * p + j):
                                first_high(n)
                        for n in second_of(y.number, 2 * p + j):
                            second_high(n)
                    if y.number == HM - 1 and p >= 5:
                        reload(p - 5)
                    if y.joint and p == 0:
                        reload(3)
                    if y.joint and 2 <= p < 6:
                        reload_out(p - 2)
            bodies(act, body)

        @block.gpsimd
        def _(pool):
            pool.memset(mhalf[:], -0.5).then_inc(mhalf_set, 1)
            pool.memset(vv[:, :, :, HD:HD + 1], 1.0).then_inc(ones_set, 1)
            pool.wait_ge(mhalf_set, 1)

            def power(src, dst, ready, done, n):
                pool.wait_ge(ready, n)
                pool.tensor_tensor(dst[:], src[:], mhalf[:], ALU.pow).then_inc(done, 1)

            def cos_sin_parts(y, p, j):
                h = 16 * y.m + 2 * p + j
                pool.wait_ge(qk_ready, h + 1)
                wait(pool, qr_ready, h - 1)
                pool.tensor_tensor(m1[:, j], qk[:, j], rope_sb[:, j, 0:1, :].broadcast_to([P, QM + 1, HD]), ALU.mult)
                half = HD // 2
                for s in range(2):
                    d, o = s * half, (1 - s) * half
                    last = pool.tensor_tensor(m2[:, j, :, d:d + half], qk[:, j, :, o:o + half],
                                              rope_sb[:, j, 1:2, d:d + half].broadcast_to([P, QM + 1, half]), ALU.mult)
                last.then_inc(m_ready, 1)

            power(veps, rstd, ve_ready, rstd_ready, 1)
            pool.wait_ge(c_in, 16 * NCONST)

            def body(y):
                for p in range(8):
                    for j in range(2):
                        if not y.drain:
                            cos_sin_parts(y, p, j)
                        if p % 4 == 0 and j == 0 and not (y.drain or y.number == NM - 1 and p == 4):
                            power(veps, rstd, ve_ready, rstd_ready, 2 * y.m + p // 4 + 2)
                        if p % 4 == 1 and j == 0 and y.old_sweep():
                            power(ve2, rs2, ve2_ready, rs2_ready, 2 * y.m - 1 + p // 4 - B)
                    a = p // 4
                    if p % 4 == 3 and not y.old_sweep() and not (y.first and a == 0) and not (y.joint and a == 1):
                        pool.wait_ge(xb_landed, 16 * (2 * y.m + a))
                        for t in range(NT):
                            last = pool.tensor_tensor(xb[:, t, :], xb[:, t, :], bo_sb[:], ALU.add)
                        last.then_inc(xb_ready, 1)
                    if y.first:
                        if p > 0:
                            pool.wait_ge(f_in, 16 * p)
                            pool.dma_start(fsum[:], factors[p], accum_op=ALU.add, max_dma_last_dim=4 * D).then_inc(f_in, 16)
                        else:
                            pool.dma_start(fsum[:], factors[0]).then_inc(f_in, 16)
                    if y.first and p == 7:
                        pool.wait_ge(tap_in, 48)
                        pool.tensor_tensor(tap0[:, 0:1], tap0[:, 0:1], tap0[:, 1:2], ALU.add).then_inc(tap_added, 1)
            bodies(pool, body)
            pool.wait_ge(f_in, 16 * RANK)

        @block.vector
        def _(dve):
            def layernorm_start(src, st, mvv, ve, chain, n, ready):
                for t in range(NT):
                    last = dve.bn_stats(st[:, t, :], src[:, t, :])
                last.then_inc(chain, 1)
                wait_apart(dve, passed, (chain, n + 1))
                for t in range(NT):
                    last = dve.bn_aggr(mvv[:, t, :], st[:, t, :])
                last.then_inc(chain, 1)
                dve.wait_ge(chain, n + 2)
                dve.tensor_scalar(ve[:], mvv[:, :, 1], EPS, None, ALU.add).then_inc(ready, 1)

            def layernorm_end(dst, src, mvv, rs, done):
                for t in range(NT):
                    dve.tensor_scalar(dst[:, t, :], src[:, t, :], mvv[:, t, 0:1], rs[:, t:t + 1],
                                      ALU.subtract, ALU.mult).then_inc(done, 1)

            def ln1_start(v):
                dve.wait_ge(x_landed, 16 * v + 16)
                layernorm_start(x_in, stats, mv, veps, ln_chain, 2 * v, ve_ready)

            def ln1_end(v):
                dve.wait_ge(rstd_ready, v + 1)
                wait(dve, xt_done, 2 * v)
                layernorm_end(xn, x_in, mv, rstd, xn_ready)

            def x_low(v, s, j):
                dve.wait_ge(xt_hi, 2 * v + j + 1)
                wait(dve, qkv_done, 8 * v - 8)
                dve.tensor_tensor(xTl[:, s, j].rearrange("p c t -> p (c t)"), tP[:, 0:D],
                                  xTh[:, s, j].rearrange("p c t -> p (c t)").bitcast(F32), ALU.subtract).then_inc(xt_lo, 1)

            def q_low(y, p, j):
                h = 16 * y.m + 2 * (p - 1) + j
                dve.wait_ge(qt_hi, h + 1)
                wait(dve, s_done, h - j - 2)
                dve.tensor_tensor(qTl[:, (p - 1) % 2, :, j * P:(j + 1) * P], tP[:, 0:3 * P].rearrange("p (c t) -> p c t", c=3),
                                  qTh[:, (p - 1) % 2, :, j * P:(j + 1) * P].bitcast(F32), ALU.subtract).then_inc(qt_lo, 1)

            def o_low(y, p):
                u = 8 * y.m + p - 4
                dve.wait_ge(ot_hi, u + 1)
                wait(dve, out_done, 2 * u - 2)
                dve.tensor_tensor(oTl[:, p % 2].rearrange("p t c n -> p (t c n)"), tP[:, 0:512],
                                  oTh[:, p % 2].rearrange("p t c n -> p (t c n)").bitcast(F32), ALU.subtract).then_inc(ot_lo, 1)

            def qkv_evac(y, p, j):
                h = 16 * y.m + 2 * p + j
                g = p % GS
                dve.wait_ge(qkv_done, h + 1)
                wait(dve, m_ready, h - 1)
                if y.joint and p < GS:
                    dve.wait_ge(w_in[g], 48)
                dve.tensor_tensor(qk[:, j].rearrange("p a d -> p (a d)"), wP[:, 0:RW], bias_sb[:, g, 0:RW],
                                  ALU.add).then_inc(qk_ready, 1)
                wait(dve, pv_done, h - j - 14)
                dve.tensor_tensor(vv[:, p, j, 0:HD], wP[:, RW:GW], bias_sb[:, g, RW:GW], ALU.add).then_inc(v_ready, 1)

            def rotate(y, u, j):
                h = 16 * y.m + 2 * u + j
                dve.wait_ge(m_ready, h + 1)
                wait(dve, qt_done, h - 1)
                dve.tensor_tensor(qr[:, j, 0:QM], m1[:, j, 0:QM], m2[:, j, 0:QM], ALU.add)
                dve.tensor_tensor(qr[:, j, QM:QM + 2], m1[:, j, QM:QM + 1].broadcast_to([P, 2, HD]),
                                  m2[:, j, QM:QM + 1].broadcast_to([P, 2, HD]), ALU.add).then_inc(qr_ready, 1)

            def mask_max(y, p, j):
                h = 16 * y.m + 2 * (p - 2) + j
                s = (2 * p + j) % 4
                wait_apart(dve, passed, (mask_landed, 16), (s_done, h + 1), (pt_done, 2 * (h - 3)), (es_ready, h - 3))
                for a in range(2):
                    for t in range(NT):
                        cols = slice(t * P, P + 2 * t * P)
                        last = dve.tensor_tensor_reduce(pr[:, s, a, cols], sP[a][:, cols], mask_sb[:, cols], 1.0, -3.0e38,
                                                        ALU.add, ALU.max, mx[:, s, 2 * a + t:2 * a + t + 1])
                last.then_inc(masked, 1)
                dve.wait_ge(masked, h + 1)
                dve.tensor_scalar(nm[:, s, :], mx[:, s, :], -SM_SCALE, None, ALU.mult).then_inc(nm_ready, 1)
                dve.wait_ge(nm_ready, h + 1)
                sweep = 0 if y.joint and p < 2 else y.sweep
                head = QM * (GS * sweep + (p - 2) % GS) + 2 * j
                dve.tensor_tensor(sk[:, s, :].rearrange("p (a t) -> p a t", a=2), nm[:, s, :].rearrange("p (a t) -> p a t", a=2),
                                  sink_sb[:, head:head + 2].unsqueeze(2).broadcast_to([P, 2, NT]), ALU.add).then_inc(sk_ready, 1)

            def normalise(y, u, j):
                h = 16 * y.m + 2 * u + j
                s = (2 * u + j) % 4
                dve.wait_ge(pv_done, h + 1)
                dve.wait_ge(es_ready, h + 1)
                v4 = vP[:].rearrange("p (c n) -> p c n", c=4)
                dve.tensor_tensor(den[:].unsqueeze(2), v4[:, :, HD:HD + 1], es[:, s, :].unsqueeze(2), ALU.add).then_inc(den_ready, 1)
                dve.wait_ge(den_ready, h + 1)
                dve.reciprocal(rden[:], den[:]).then_inc(rden_ready, 1)
                dve.wait_ge(rden_ready, h + 1)
                if j == 0:
                    wait(dve, ot_done, 8 * y.m + u - 1)
                dve.tensor_tensor(o_sb[:, u % 2, :, 2 * j:2 * j + 2, :].rearrange("p t a d -> p a t d"),
                                  vP[:].rearrange("p (a t n) -> p a t n", a=2, t=2)[:, :, :, 0:HD],
                                  rden[:].rearrange("p (a t) -> p a t", a=2).unsqueeze(3).broadcast_to([P, 2, NT, HD]),
                                  ALU.mult).then_inc(o_ready, 1)

            def residual(y, a, t):
                v = 2 * y.m - 2 + a
                late = y.old_sweep()
                if late:
                    dve.wait_ge(xb_landed, 16 * v + 16)
                else:
                    dve.wait_ge(xb_ready, v + 1)
                dve.wait_ge(out_done, 8 * v + 7 + t)
                wait(dve, x1_stored, 16 * v)
                dve.tensor_tensor(x1[:, t, :], oP[t][:], xb[:, t, :], ALU.add).then_inc(x1_ready, 1)
                if late and t == NT - 1:
                    dve.wait_ge(x1_ready, 2 * v + 2)
                    layernorm_start(x1, st2, mv2, ve2, ln2_chain, 2 * (v - B), ve2_ready)

            def ln2_end(y, a):
                v = 2 * y.m - 2 + a - B
                dve.wait_ge(rs2_ready, v + 1)
                wait(dve, x1t_done, 2 * v)
                layernorm_end(x1n, x1, mv2, rs2, x1n_ready)

            dve.wait_ge(mhalf_set, 1)
            ln1_start(0)
            ln1_end(0)

            def first_low(n):
                c = first_chunks[n]
                width = raw_of(c)[1]
                dve.wait_ge(hi_done, n + 1)
                dve.tensor_tensor(placed(c, wl, wol), work[:, (n % 3) * CHUNK:(n % 3) * CHUNK + width],
                                  placed(c, wh, woh).bitcast(F32), ALU.subtract).then_inc(lo_done, 1)

            for n in range(FIRST_PEELED):
                first_low(n)
                if n < NT:
                    x_low(0, 0, n)
            dve.wait_ge(c_in, 16 * NCONST)
            dve.wait_ge(ones_set, 1)

            def second_low(n):
                width = raw_of(second_chunks[n])[1]
                dve.wait_ge(hi_done, NF + n + 1)
                dve.tensor_tensor(work[:, 2 * CHUNK:2 * CHUNK + width].bitcast(F32R), work[:, 0:width],
                                  work[:, CHUNK:CHUNK + width], ALU.subtract).then_inc(lo_done, 1)

            def body(y):
                for p in range(8):
                    for j in range(2):
                        u, jj = (p - 1, 1) if j == 0 else (p, 0)
                        if y.here(u, 0):
                            rotate(y, u, jj)
                        if not y.drain:
                            qkv_evac(y, p, j)
                        if y.here(p, 1):
                            q_low(y, p, j)
                        if y.here(p, 2):
                            mask_max(y, p, j)
                        if x_next(y, p, j):
                            x_low(2 * y.m + p // 4 + 1, (p // 4 + 1) % 2, p % 4 - 1)
                        if j == 1 and y.here(p, 4):
                            o_low(y, p)
                        u, jj = (p - 4, 1) if j == 0 else (p - 3, 0)
                        if y.here(u, 0):
                            normalise(y, u, jj)
                        if p % 4 == 0 and not (y.drain or y.number == NM - 1 and p == 4):
                            if j == 0:
                                ln1_start(2 * y.m + p // 4 + 1)
                            else:
                                ln1_end(2 * y.m + p // 4 + 1)
                        if not y.first:
                            if p % 4 == j ^ 1 and p % 4 < 2:
                                residual(y, p // 4, 1 - j)
                            if p % 4 == 1 and j == 1 and y.old_sweep():
                                ln2_end(y, p // 4)
                        if y.first:
                            for n in first_of(2 * p + j):
                                first_low(n)
                        for n in second_of(y.number, 2 * p + j):
                            second_low(n)
            bodies(dve, body)


def conv_part(nc, ctx_in, pad_dram, q2_dram, big):
    with ExitStack() as ctx:
        def sb(name, shape):
            return ctx.enter_context(nc.sbuf_tensor(name, shape, F32))

        def sem(name):
            return ctx.enter_context(nc.semaphore(name))

        kk = sb("kk", [P, 2, KD, 12, BG])
        tap = sb("tap", [P, 2, D])
        kv = sb("kv", [P, 2, KD, NY])
        qs = sb("qs", [P, 2, KD, 12, BG])
        terms = sb("terms", [P, 2, KD, 8 * 8 * BG])
        res = sb("res", [P, 2, KD, CD * BG])
        y = ctx.enter_context(nc.psum_tensor("y", [P, 2, KD, 512], F32))

        conv_passed = sem("conv_passed")
        q_landed = [sem(f"q_landed{g}") for g in range(NBG)]
        kk_landed = [sem(f"kk_landed{i}") for i in range(2)]
        tap_landed = [sem(f"tap_landed{i}") for i in range(2)]
        kv_ready = sem("kv_ready")
        qs_ready = sem("qs_ready")
        conv_done = sem("conv_done")
        terms_ready = sem("terms_ready")
        res_ready = sem("res_ready")
        res_placed = sem("res_placed")
        block = ctx.enter_context(nc.Block())

        def units(eng, body):
            for bg in range(NBG):
                base = bg * CH
                if bg == 0:
                    body(0, 0, bg, 0)
                    body(1, 1, bg, 1)
                with eng.Fori(1 if bg == 0 else 0, CH // 2) as i:
                    for s in range(2):
                        body(base + 2 * i + s, 2 * i + s, bg, s)

        def wait(eng, s, value):
            if isinstance(value, int) and value <= 0:
                return
            eng.wait_ge(s, value)

        @block.sync
        def _(sp):
            def body(u, h, bg, s):
                wait(sp, kv_ready, u - 1)
                sp.dma_start(kk[:, s], ctx_in[bg, h]).then_inc(kk_landed[s], 16)
                wait(sp, conv_done, u - 1)
                sp.dma_start(tap[:, s], bass.AP(tensor=pad_dram.tensor, offset=h * PADW, ap=[[1, P], [1, D]]))\
                  .then_inc(tap_landed[s], 16)
                if isinstance(u, int) and u == 0:
                    for b in range(BG):
                        sp.dma_start(big[:, b], q2_dram[b]).then_inc(q_landed[0], 16)
            units(sp, body)

        @block.gpsimd
        def _(pool):
            def body(u, h, bg, s):
                pool.wait_ge(kk_landed[s], 8 * (u - s) + 16)
                wait(pool, conv_done, u - 1)
                n = 8 * BG
                k0 = kk[:, s, :, 0:8, :].rearrange("p c i b -> p c (i b)")
                row = k0.ap[1][0]
                shifted = bass.AP(tensor=k0.tensor, offset=k0.offset, ap=[list(k0.ap[0]), [row, KD], [BG, 4], [1, n]])
                pool.tensor_tensor(kv[:, s, :, 0:4 * n].rearrange("p c (d n) -> p c d n", d=4),
                                   k0.unsqueeze(2).broadcast_to([P, KD, 4, n]), shifted, ALU.mult)
                pool.tensor_tensor(kv[:, s, :, 4 * n:NY],
                                   kk[:, s, :, 0:4, :].rearrange("p c i b -> p c (i b)"),
                                   kk[:, s, :, 4:8, :].rearrange("p c i b -> p c (i b)"), ALU.mult).then_inc(kv_ready, 1)
            units(pool, body)

        @block.scalar
        def _(act):
            def fetch(u, h, bg, s):
                wait_apart(act, conv_passed, (q_landed[bg], 16 * BG), (terms_ready, u - 1))
                mine = big[:, bg * BG:(bg + 1) * BG, :, :]
                act.copy(qs[:, s, :, 0:8, :], mine[:, :, :, bass.ds(h * CD, 8)].rearrange("p b c i -> p c i b"))
                act.copy(qs[:, s, :, 8:12, :], mine[:, :, :, bass.ds(h * CD, 4)].rearrange("p b c i -> p c i b")).then_inc(qs_ready, 1)

            def place(u, h, bg, s):
                wait_apart(act, conv_passed, (q_landed[bg], 16 * BG), (res_ready, u + 1))
                act.copy(big[:, bg * BG:(bg + 1) * BG, :, bass.ds(h * CD, CD)].rearrange("p b c i -> p c i b"),
                         res[:, s].rearrange("p c (i b) -> p c i b", i=CD)).then_inc(res_placed, 1)

            for bg in range(NBG):
                base = bg * CH
                fetch(base, 0, bg, 0)
                if bg == 0:
                    for b in range(BG, B):
                        act.dma_start(big[:, b], q2_dram[b]).then_inc(q_landed[1], 16)
                    fetch(1, 1, bg, 1)
                    place(0, 0, bg, 0)
                    fetch(2, 2, bg, 0)
                    place(1, 1, bg, 1)
                with act.Fori(1 if bg == 0 else 0, CH // 2 - 1) as i:
                    for s in range(2):
                        fetch(base + 2 * i + s + 1, 2 * i + s + 1, bg, 1 - s)
                        place(base + 2 * i + s, 2 * i + s, bg, s)
                fetch(base + CH - 1, CH - 1, bg, 1)
                place(base + CH - 2, CH - 2, bg, 0)
                place(base + CH - 1, CH - 1, bg, 1)

        @block.tensor
        def _(pe):
            def body(u, h, bg, s):
                pe.wait_ge(tap_landed[s], 8 * (u - s) + 16)
                pe.wait_ge(kv_ready, u + 1)
                wait(pe, terms_ready, u - 1)
                for d in range(KD):
                    for c in range(d, KD):
                        last = pe.matmul(y[:, s, c, 0:NY], tap[:, s, d * P:(d + 1) * P], kv[:, s, c - d, :],
                                         start=(d == 0), stop=(d == c))
                last.then_inc(conv_done, 1)
            units(pe, body)

        @block.vector
        def _(dve):
            n = CD * BG

            def body(u, h, bg, s):
                dve.wait_ge(qs_ready, u + 1)
                dve.wait_ge(conv_done, u + 1)
                wait(dve, res_ready, u - 1)
                yy = y[:, s, :, 0:NY]
                q0 = qs[:, s, :, 0:8, :].rearrange("p c i b -> p c (i b)")
                tt = terms[:, s]
                part = tt.ap[0]
                row = [8 * n, KD]

                def at(first, *dims):
                    return bass.AP(tensor=tt.tensor, offset=tt.offset + first, ap=[list(part), row, *dims])

                dve.tensor_tensor(at(0, [n + BG, 4], [1, n]), yy[:, :, 0:4 * n].rearrange("p c (d n) -> p c d n", d=4),
                                  q0.unsqueeze(2).broadcast_to([P, KD, 4, n]), ALU.mult)
                dve.tensor_tensor(at(4 * n + 4 * BG, [1, 4 * BG]), yy[:, :, 4 * n:NY], q0[:, :, 0:4 * BG], ALU.mult)
                dve.tensor_tensor(at(n, [n + BG, 4], [1, BG]), yy[:, :, 4 * n:NY].rearrange("p c (a b) -> p c a b", a=4),
                                  qs[:, s, :, 4:8, :], ALU.mult)
                qd = qs[:, s, :, 1:2, :]
                shifted = bass.AP(tensor=qd.tensor, offset=qd.offset, ap=[list(qd.ap[0]), [12 * BG, KD], [BG, 3], [1, n]])
                dve.tensor_tensor(at(5 * n, [n, 3], [1, n]), yy[:, :, n:4 * n].rearrange("p c (d n) -> p c d n", d=3),
                                  shifted, ALU.mult).then_inc(terms_ready, 1)
                dve.wait_ge(terms_ready, u + 1)
                wait(dve, res_placed, u - 1)
                dve.tensor_reduce(res[:, s], at(0, [1, n], [n, 8]), AX.X, ALU.add).then_inc(res_ready, 1)
            units(dve, body)


def mix_part(nc, x1_dram, big, bias, ident, fsum, out):
    NV = B * NT
    with ExitStack() as ctx:
        def sb(name, shape, dt=F32):
            return ctx.enter_context(nc.sbuf_tensor(name, shape, dt))

        def sem(name):
            return ctx.enter_context(nc.semaphore(name))

        def ps(name):
            return [ctx.enter_context(nc.psum_tensor(f"{name}{t}", [P, 512], F32)) for t in range(NT)]

        id3 = sb("id3", [P, P])
        bias3 = sb("bias3", [P, D])
        stage = sb("stage", [P, 2, KD, T])
        xr = sb("xr", [P, 2, NT, D])
        x2 = sb("x2", [P, NT, D])
        x2b = sb("x2b", [P, 4, D])
        xn3 = sb("xn3", [P, NT, D])
        nTh = sb("nTh", [P, NT, KD, P], F32R)
        nTl = sb("nTl", [P, NT, KD, P], F32R)
        fh = sb("fh", [P, KD, D], F32R)
        fl = sb("fl", [P, KD, D], F32R)
        st3 = sb("st3", [P, NT, 6])
        mv3 = sb("mv3", [P, NT, 2])
        ve3 = sb("ve3", [P, NT])
        rs3 = sb("rs3", [P, NT])
        mhalf3 = sb("mhalf3", [P, NT])
        fin = sb("fin", [P, NT, D])
        aP, nP, fP = ps("aP"), ps("nP"), ps("fP")

        mix_passed = sem("mix_passed")
        const_in = sem("const_in")
        bias_in = sem("bias_in")
        half_set = sem("half_set")
        staged = [sem(f"staged{m}") for m in range(2)]
        xr_landed = [sem(f"xr_landed{m}") for m in range(2)]
        a_done = sem("a_done")
        x2_ready = sem("x2_ready")
        chain3 = sem("chain3")
        ve3_ready = sem("ve3_ready")
        rs3_ready = sem("rs3_ready")
        x2b_ready = sem("x2b_ready")
        xn3_ready = sem("xn3_ready")
        n_done = sem("n_done")
        n_hi = sem("n_hi")
        n_lo = sem("n_lo")
        f_hi = sem("f_hi")
        f_lo = sem("f_lo")
        f_done = sem("f_done")
        fin_ready = sem("fin_ready")
        stored = [sem(f"stored{t}") for t in range(NT)]
        block = ctx.enter_context(nc.Block())

        def wait(eng, s, value):
            if isinstance(value, int) and value <= 0:
                return
            eng.wait_ge(s, value)

        def steps(eng, body, lag=2):
            for v in range(4):
                body(v, v)
            with eng.Fori(1, NV // 4) as i:
                for w in range(4):
                    body(4 * i + w, w)
            for v in range(NV, NV + lag):
                body(v, v % 4)

        def has(v, lag):
            return not isinstance(v, int) or 0 <= v - lag < NV

        @block.sync
        def _(sp):
            sp.dma_start(id3[:], ident).then_inc(const_in, 16)

            def load(v, b, m):
                wait(sp, a_done, v - 2)
                sp.dma_start(stage[:, m], big[:, b]).then_inc(staged[m], 16)
                wait(sp, x2_ready, v - 2)
                sp.dma_start(xr[:, m], x1_dram[b].rearrange("(t p) d -> p t d", p=P)).then_inc(xr_landed[m], 16)

            load(0, 0, 0)
            sp.dma_start(bias3[:], bias.partition_broadcast(P)).then_inc(bias_in, 16)
            load(2, 1, 1)
            with sp.Fori(1, NV // 4) as i:
                for m in range(2):
                    load(4 * i + 2 * m, 2 * i + m, m)

        @block.scalar
        def _(act):
            def evac(v, t):
                act.wait_ge(n_done, v + 1)
                wait(act, f_done, v - 1)
                act.copy(nTh[:, t], nP[t][:].rearrange("p (c n) -> p c n", c=KD)).then_inc(n_hi, 1)

            for c in range(KD):
                act.copy(fh[:, c], fsum[:, c]).then_inc(f_hi, 1)

            def store(v, t, row):
                act.wait_ge(fin_ready, v + 1)
                act.dma_start(row, fin[:, t]).then_inc(stored[t], 16)

            rows = out.rearrange("b (t p) d -> (b t) p d", p=P)

            def body(v, w):
                t = w % 2
                if has(v, 1):
                    evac(v - 1, 1 - t)
                if has(v, 3):
                    store(v - 3, 1 - t, rows[v - 3])
            steps(act, body, lag=3)
            for t in range(NT):
                act.wait_ge(stored[t], 8 * NV)

        @block.gpsimd
        def _(pool):
            pool.memset(mhalf3[:], -0.5).then_inc(half_set, 1)
            pool.wait_ge(half_set, 1)
            pool.wait_ge(bias_in, 16)

            def body(v, w):
                t = w % 2
                if has(v, 0):
                    pool.wait_ge(ve3_ready, v + 1)
                    pool.tensor_tensor(rs3[:, t:t + 1], ve3[:, t:t + 1], mhalf3[:, t:t + 1], ALU.pow).then_inc(rs3_ready, 1)
                    wait(pool, fin_ready, v - 3)
                    pool.tensor_tensor(x2b[:, w], x2[:, t], bias3[:], ALU.add).then_inc(x2b_ready, 1)
            steps(pool, body, lag=0)

        @block.tensor
        def _(pe):
            pe.wait_ge(const_in, 16)

            def body(v, w):
                t, m = w % 2, w // 2
                if has(v, 0):
                    pe.wait_ge(staged[m], 4 * (v - w) + 16)
                    wait(pe, x2_ready, v - 1)
                    for c in range(KD):
                        last = pe.transpose(aP[t][:, c * P:(c + 1) * P], stage[:, m, c, t * P:(t + 1) * P], id3[:])
                    last.then_inc(a_done, 1)
                if has(v, 1):
                    pe.wait_ge(xn3_ready, v)
                    wait(pe, n_lo, v - 2)
                    for c in range(KD):
                        last = pe.transpose(nP[1 - t][:, c * P:(c + 1) * P], xn3[:, 1 - t, c * P:(c + 1) * P], id3[:])
                    last.then_inc(n_done, 1)
                if has(v, 2):
                    pe.wait_ge(n_lo, v - 1)
                    if isinstance(v, int) and v == 2:
                        pe.wait_ge(f_lo, KD)
                    wait(pe, fin_ready, v - 3)
                    for c in range(KD):
                        for n, (a, f) in enumerate([(nTh, fh), (nTl, fh), (nTh, fl)]):
                            last = pe.matmul(fP[t][:], a[:, t, c, :], f[:, c, :], start=(c == 0 and n == 0), stop=(c == KD - 1 and n == 2))
                    last.then_inc(f_done, 1)
            steps(pe, body)

        @block.vector
        def _(dve):
            def body(v, w):
                t, m = w % 2, w // 2
                if has(v, 0):
                    dve.wait_ge(xr_landed[m], 4 * (v - w) + 16)
                    dve.wait_ge(a_done, v + 1)
                    wait(dve, x2b_ready, v - 1)
                    dve.tensor_tensor(x2[:, t], aP[t][:], xr[:, m, t], ALU.add).then_inc(x2_ready, 1)
                    dve.wait_ge(x2_ready, v + 1)
                    dve.bn_stats(st3[:, t], x2[:, t]).then_inc(chain3, 1)
                    wait_apart(dve, mix_passed, (chain3, 2 * v + 1))
                    dve.bn_aggr(mv3[:, t], st3[:, t]).then_inc(chain3, 1)
                    dve.wait_ge(chain3, 2 * v + 2)
                    dve.tensor_scalar(ve3[:, t:t + 1], mv3[:, t, 1:2], EPS, None, ALU.add).then_inc(ve3_ready, 1)
                if has(v, 3):
                    dve.wait_ge(f_done, v - 2)
                    dve.wait_ge(x2b_ready, v - 2)
                    wait(dve, stored[1 - t], 8 * (v - 3 - (1 - t)))
                    dve.scalar_tensor_tensor(fin[:, 1 - t], fP[1 - t][:], 1.0 / math.sqrt(RANK), x2b[:, (w + 1) % 4],
                                             ALU.mult, ALU.add).then_inc(fin_ready, 1)
                if has(v, 0):
                    dve.wait_ge(rs3_ready, v + 1)
                    wait(dve, n_done, v - 1)
                    dve.tensor_scalar(xn3[:, t], x2[:, t], mv3[:, t, 0:1], rs3[:, t:t + 1],
                                      ALU.subtract, ALU.mult).then_inc(xn3_ready, 1)
                if has(v, 1):
                    dve.wait_ge(n_hi, v)
                    dve.tensor_tensor(nTl[:, 1 - t], nP[1 - t][:].rearrange("p (c n) -> p c n", c=KD),
                                      nTh[:, 1 - t].bitcast(F32), ALU.subtract).then_inc(n_lo, 1)
                if isinstance(v, int) and v == 0:
                    for c in range(KD):
                        dve.wait_ge(f_hi, c + 1)
                        dve.tensor_tensor(fl[:, c], fsum[:, c], fh[:, c].bitcast(F32), ALU.subtract).then_inc(f_lo, 1)
            steps(dve, body, lag=3)


def decoder_layer(nc, x, ctxt, wqkv, bqkv, wout, bout, sinks, ssm_pad, dcoef, factors, bias, rope, masks, ident, out):
    x1_dram = nc.dram_tensor("x1_rows", [B, T, D], F32).ap()
    q2_dram = nc.dram_tensor("q2_cols", [B, P, KD, T], F32).ap()
    pad_dram = nc.dram_tensor("padded_taps", [CH, PADW], F32).ap()
    with nc.sbuf_tensor("fsum", [P, KD, D], F32) as fsum:
        attention_part(nc, x, wqkv, bqkv, wout, bout, sinks, rope, masks, ident, factors, ssm_pad, dcoef,
                       x1_dram, q2_dram, pad_dram, fsum)
        with nc.sbuf_tensor("big", [P, B, KD, T], F32) as big:
            conv_part(nc, ctxt, pad_dram, q2_dram, big)
            mix_part(nc, x1_dram, big, bias, ident, fsum, out)


def layout(inputs):
    a = {k: np.asarray(v) for k, v in inputs.items()}
    wq, bq = a["L0_attn_qkv_w"], a["L0_attn_qkv_b"]
    nq, nk = NH * HD, NKV * HD
    w = np.concatenate([wq[:nq].reshape(NKV, QM * HD, D), wq[nq:nq + nk].reshape(NKV, HD, D),
                        wq[nq + nk:].reshape(NKV, HD, D)], axis=1)
    bias = np.concatenate([bq[:nq].reshape(NKV, QM * HD), bq[nq:nq + nk].reshape(NKV, HD),
                           bq[nq + nk:].reshape(NKV, HD)], axis=1)
    c = a["ctx_2048"].reshape(NBG, BG, CH, CD, KD, P)[..., ::-1].transpose(0, 2, 5, 4, 3, 1)
    c = np.concatenate([c, c[:, :, :, :, 0:4]], axis=4)
    return {
        "x": a["x"],
        "ctxt": np.ascontiguousarray(c),
        "ssm_pad": np.ascontiguousarray(np.pad(a["L0_xattn_ssm_kernel"], [(0, 0), (P - 1, 1)])),
        "dcoef": a["L0_xattn_D"].reshape(CH, 1),
        "factors": np.ascontiguousarray(a["L0_ffn_factors"].reshape(RANK, KD, P, D).transpose(0, 2, 1, 3)),
        "bias": a["L0_ffn_bias"],
        "wqkv": np.ascontiguousarray(w.reshape(NKV, GW, KD, P).transpose(3, 2, 0, 1)),
        "bqkv": np.ascontiguousarray(bias.reshape(-1)),
        "wout": np.ascontiguousarray(a["L0_attn_out_w"].reshape(D, NH * HD // P, P).transpose(2, 1, 0)),
        "bout": a["L0_attn_out_b"],
        "sinks": a["L0_attn_sinks"],
        "rope": rope_tables(),
        "masks": score_masks(),
        "ident": np.eye(P, dtype=np.float32),
    }


def kernel(**inputs):
    import concourse.bacc as bacc
    from concourse.bass_utils import run_bass_kernel_spmd

    nc = bacc.Bacc("TRN2", target_bir_lowering=False, num_devices=1)
    arrays = layout(inputs)
    args = {name: nc.dram_tensor(f"in_{name}", a.shape, mybir.dt.from_np(a.dtype), kind="ExternalInput").ap()
            for name, a in arrays.items()}
    out = nc.dram_tensor("out_rows", [B, T, D], F32, kind="ExternalOutput").ap()
    decoder_layer(nc, out=out, **args)
    r = run_bass_kernel_spmd(nc, [{f"in_{name}": a for name, a in arrays.items()}], core_ids=[0])
    return r.results[0]["out_rows"]
```
